# Optimizing a Trainium2 kernel written in Bass

```python
import numpy as np
import jax
import jax.numpy as jnp

def _softmax(x, axis=-1):
    return jax.nn.softmax(x, axis=axis)

def _gelu(x):
    return jax.nn.gelu(x, approximate=True)

def _silu(x):
    return jax.nn.silu(x)

def _sigmoid(x):
    return jax.nn.sigmoid(x)

def _layernorm(x, axis=-1, eps=1e-05):
    m = jnp.mean(x, axis=axis, keepdims=True)
    v = jnp.var(x, axis=axis, keepdims=True)
    return (x - m) / jnp.sqrt(v + eps)

def _scatter_add(tgt, idx, src, axis=0):
    return tgt.at[idx].add(src)

def _segment_sum(src, seg, n):
    return jax.ops.segment_sum(src, seg, n)
kernel_name = 'mk_gnn_preln_d4_gnn_r8_44f73b'

def setup_inputs(seed: int=0):
    np.random.seed(seed)
    _w = jnp.asarray

    def _rec_inputs():
        import jax
        import jax.numpy as jnp
        _gk = jax.random.key(seed)
        x = -8.776e-05 + 1 * jax.random.normal(jax.random.fold_in(_gk, 1), (5000, 128), jnp.float32)
        src = jax.random.randint(jax.random.fold_in(_gk, 2), (80000,), 0, 5000, jnp.int32)
        dst = jax.random.randint(jax.random.fold_in(_gk, 3), (80000,), 0, 5000, jnp.int32)
        _o = jnp.argsort(dst, stable=True)
        src = src[_o]
        dst = dst[_o]
        edge_attr_32 = 0.000279952 + 1.00013 * jax.random.normal(jax.random.fold_in(_gk, 12), (80000, 32), jnp.float32)
        edge_type_8 = jax.random.randint(jax.random.fold_in(_gk, 14), (80000,), 0, 8, jnp.int32)
        edge_weight = jax.random.uniform(jax.random.fold_in(_gk, 15), (80000,), jnp.float32, 0.0, 1)
        return (x, src, dst, edge_attr_32, edge_type_8, edge_weight)
    x, src, dst, edge_attr_32, edge_type_8, edge_weight = _rec_inputs()

    def _L0_gnn_setup():
        import jax, jax.numpy as jnp
        import numpy as np
        N, E = (5000, 80000)
        DIN, C, EDIM = (128, 128, 32)
        key = jax.random.key(seed)
        ks = jax.random.split(key, 9)
        x = jax.random.normal(ks[0], (N, DIN), dtype=jnp.float32)
        edge_index = jax.random.randint(ks[1], (2, E), 0, N, dtype=jnp.int64)
        edge_attr = jax.random.normal(ks[2], (E, EDIM), dtype=jnp.float32)
        s = 1.0 / np.sqrt(DIN)
        W = jax.random.normal(ks[3], (DIN, C), dtype=jnp.float32) * s
        W_edge = jax.random.normal(ks[4], (EDIM, C), dtype=jnp.float32) / np.sqrt(EDIM)
        att_src = jax.random.normal(ks[5], (C,), dtype=jnp.float32) * s
        att_dst = jax.random.normal(ks[6], (C,), dtype=jnp.float32) * s
        att_edge = jax.random.normal(ks[7], (C,), dtype=jnp.float32) * s
        bias = jnp.zeros((C,), dtype=jnp.float32)
        return {'x': x, 'edge_index': edge_index, 'edge_attr': edge_attr, 'W': W, 'W_edge': W_edge, 'att_src': att_src, 'att_dst': att_dst, 'att_edge': att_edge, 'bias': bias}
    _L0_gnn_all = _L0_gnn_setup()
    _L0_gnn_in = {k: v for k, v in _L0_gnn_all.items() if k in ('W', 'W_edge', 'att_src', 'att_dst', 'att_edge', 'bias')}
    del _L0_gnn_all

    def _L1_gnn_setup():
        import jax, jax.numpy as jnp
        import numpy as np
        N_NODES = 12500
        N_EDGES = 400000
        D_IN = 128
        D_OUT = 128
        key = jax.random.key(seed)
        k1, k2, k3, k4, k5, k6 = jax.random.split(key, 6)
        x = jax.random.normal(k1, (N_NODES, D_IN), dtype=jnp.float32)
        edge_row = jax.random.randint(k2, (N_EDGES,), 0, N_NODES, dtype=jnp.int64 if jax.config.jax_enable_x64 else jnp.int32)
        edge_col = jax.random.randint(k3, (N_EDGES,), 0, N_NODES, dtype=jnp.int64 if jax.config.jax_enable_x64 else jnp.int32)
        edge_val = jax.random.uniform(k4, (N_EDGES,), dtype=jnp.float32)
        stdv = 1.0 / np.sqrt(D_OUT)
        weight = jax.random.uniform(k5, (D_IN, D_OUT), minval=-stdv, maxval=stdv, dtype=jnp.float32)
        bias = jax.random.uniform(k6, (D_OUT,), minval=-stdv, maxval=stdv, dtype=jnp.float32)
        return {'x': x, 'edge_row': edge_row, 'edge_col': edge_col, 'edge_val': edge_val, 'weight': weight, 'bias': bias}
    _L1_gnn_all = _L1_gnn_setup()
    _L1_gnn_in = {k: v for k, v in _L1_gnn_all.items() if k in ('weight', 'bias')}
    del _L1_gnn_all

    def _L2_gnn_setup():
        import jax, jax.numpy as jnp
        import numpy as np
        N_NODES = 6250
        N_EDGES = 100000
        D_IN, D_HID, D_OUT = (128, 256, 128)

        def _sage_conv(x, src, dst, W_l, b_l, W_r, num_nodes):
            msgs = x[src]
            agg_sum = jax.ops.segment_sum(msgs, dst, num_segments=num_nodes)
            deg = jax.ops.segment_sum(jnp.ones((src.shape[0],), x.dtype), dst, num_segments=num_nodes)
            agg = agg_sum / jnp.maximum(deg, 1.0)[:, None]
            return agg @ W_l.T + b_l + x @ W_r.T
        key = jax.random.key(seed)
        ks = jax.random.split(key, 10)
        s = lambda d: 1.0 / np.sqrt(d)
        return {'node_features': jax.random.normal(ks[0], (N_NODES, D_IN), jnp.float32), 'edge_index': jax.random.randint(ks[1], (2, N_EDGES), 0, N_NODES, jnp.int64), 'W_l1': jax.random.normal(ks[2], (D_HID, D_IN), jnp.float32) * s(D_IN), 'b_l1': jnp.zeros((D_HID,), jnp.float32), 'W_r1': jax.random.normal(ks[3], (D_HID, D_IN), jnp.float32) * s(D_IN), 'W_l2': jax.random.normal(ks[4], (D_HID, D_HID), jnp.float32) * s(D_HID), 'b_l2': jnp.zeros((D_HID,), jnp.float32), 'W_r2': jax.random.normal(ks[5], (D_HID, D_HID), jnp.float32) * s(D_HID), 'W_l3': jax.random.normal(ks[6], (D_OUT, D_HID), jnp.float32) * s(D_HID), 'b_l3': jnp.zeros((D_OUT,), jnp.float32), 'W_r3': jax.random.normal(ks[7], (D_OUT, D_HID), jnp.float32) * s(D_HID), 'W_proj': jax.random.normal(ks[8], (D_OUT, D_HID), jnp.float32) * s(D_HID)}
    _L2_gnn_all = _L2_gnn_setup()
    _L2_gnn_in = {k: v for k, v in _L2_gnn_all.items() if k in ('W_l1', 'b_l1', 'W_r1', 'W_l2', 'b_l2', 'W_r2', 'W_l3', 'b_l3', 'W_r3', 'W_proj')}
    del _L2_gnn_all

    def _L3_gnn_setup():
        import jax, jax.numpy as jnp
        import numpy as np
        IN_CH, HID_CH, OUT_CH, NUM_REL = (128, 256, 128, 8)
        N_NODES, N_EDGES = (6250, 100000)

        def _glorot(key, shape):
            fan_in, fan_out = (shape[-2], shape[-1])
            lim = float(np.sqrt(6.0 / (fan_in + fan_out)))
            return jax.random.uniform(key, shape, jnp.float32, -lim, lim)

        def _rgcn_conv(x, src, dst, etype, W, root, b):
            n, d = x.shape
            r = W.shape[0]
            seg = dst.astype(jnp.int32) * r + etype.astype(jnp.int32)
            msg = x[src]
            agg = jax.ops.segment_sum(msg, seg, num_segments=n * r)
            cnt = jax.ops.segment_sum(jnp.ones((msg.shape[0],), x.dtype), seg, num_segments=n * r)
            mean = agg / jnp.maximum(cnt, 1.0)[:, None]
            mean = mean.reshape(n, r, d)
            out = jnp.einsum('nrd,rdo->no', mean, W) + x @ root + b
            return out
        key = jax.random.key(seed)
        ks = jax.random.split(key, 12)
        x = jax.random.normal(ks[0], (N_NODES, IN_CH), jnp.float32)
        edge_index = jax.random.randint(ks[1], (2, N_EDGES), 0, N_NODES, jnp.int32)
        edge_type = jax.random.randint(ks[2], (N_EDGES,), 0, NUM_REL, jnp.int32)
        return {'x': x, 'edge_index': edge_index, 'edge_type': edge_type, 'W1': _glorot(ks[3], (NUM_REL, IN_CH, HID_CH)), 'root1': _glorot(ks[4], (IN_CH, HID_CH)), 'b1': jnp.zeros((HID_CH,), jnp.float32), 'W2': _glorot(ks[5], (NUM_REL, HID_CH, HID_CH)), 'root2': _glorot(ks[6], (HID_CH, HID_CH)), 'b2': jnp.zeros((HID_CH,), jnp.float32), 'W3': _glorot(ks[7], (NUM_REL, HID_CH, OUT_CH)), 'root3': _glorot(ks[8], (HID_CH, OUT_CH)), 'b3': jnp.zeros((OUT_CH,), jnp.float32)}
    _L3_gnn_all = _L3_gnn_setup()
    _L3_gnn_in = {k: v for k, v in _L3_gnn_all.items() if k in ('W1', 'root1', 'b1', 'W2', 'root2', 'b2', 'W3', 'root3', 'b3')}
    del _L3_gnn_all
    return {'x': x, 'src': src, 'dst': dst, 'edge_attr_32': edge_attr_32, 'edge_type_8': edge_type_8, 'edge_weight': edge_weight, 'L0_gnn_W': _L0_gnn_in['W'], 'L0_gnn_W_edge': _L0_gnn_in['W_edge'], 'L0_gnn_att_src': _L0_gnn_in['att_src'], 'L0_gnn_att_dst': _L0_gnn_in['att_dst'], 'L0_gnn_att_edge': _L0_gnn_in['att_edge'], 'L0_gnn_bias': _L0_gnn_in['bias'], 'L1_gnn_weight': _L1_gnn_in['weight'], 'L1_gnn_bias': _L1_gnn_in['bias'], 'L2_gnn_W_l1': _L2_gnn_in['W_l1'], 'L2_gnn_b_l1': _L2_gnn_in['b_l1'], 'L2_gnn_W_r1': _L2_gnn_in['W_r1'], 'L2_gnn_W_l2': _L2_gnn_in['W_l2'], 'L2_gnn_b_l2': _L2_gnn_in['b_l2'], 'L2_gnn_W_r2': _L2_gnn_in['W_r2'], 'L2_gnn_W_l3': _L2_gnn_in['W_l3'], 'L2_gnn_b_l3': _L2_gnn_in['b_l3'], 'L2_gnn_W_r3': _L2_gnn_in['W_r3'], 'L2_gnn_W_proj': _L2_gnn_in['W_proj'], 'L3_gnn_W1': _L3_gnn_in['W1'], 'L3_gnn_root1': _L3_gnn_in['root1'], 'L3_gnn_b1': _L3_gnn_in['b1'], 'L3_gnn_W2': _L3_gnn_in['W2'], 'L3_gnn_root2': _L3_gnn_in['root2'], 'L3_gnn_b2': _L3_gnn_in['b2'], 'L3_gnn_W3': _L3_gnn_in['W3'], 'L3_gnn_root3': _L3_gnn_in['root3'], 'L3_gnn_b3': _L3_gnn_in['b3']}

def reference(x, src, dst, edge_attr_32, edge_type_8, edge_weight, L0_gnn_W, L0_gnn_W_edge, L0_gnn_att_src, L0_gnn_att_dst, L0_gnn_att_edge, L0_gnn_bias, L1_gnn_weight, L1_gnn_bias, L2_gnn_W_l1, L2_gnn_b_l1, L2_gnn_W_r1, L2_gnn_W_l2, L2_gnn_b_l2, L2_gnn_W_r2, L2_gnn_W_l3, L2_gnn_b_l3, L2_gnn_W_r3, L2_gnn_W_proj, L3_gnn_W1, L3_gnn_root1, L3_gnn_b1, L3_gnn_W2, L3_gnn_root2, L3_gnn_b2, L3_gnn_W3, L3_gnn_root3, L3_gnn_b3):
    import jax
    import jax.numpy as jnp

    def _L0_gnn_ref(x, edge_index, edge_attr, W, W_edge, att_src, att_dst, att_edge, bias):
        import jax, jax.numpy as jnp
        import numpy as np
        N, E = (5000, 80000)
        DIN, C, EDIM = (128, 128, 32)
        h = x @ W
        a_src = h @ att_src
        a_dst = h @ att_dst
        src, dst = (edge_index[0], edge_index[1])
        e = edge_attr @ W_edge
        a_edge = e @ att_edge
        alpha = a_src[src] + a_dst[dst] + a_edge
        alpha = jax.nn.leaky_relu(alpha, negative_slope=0.2)
        amax = jax.ops.segment_max(alpha, dst, num_segments=N)
        amax = jnp.where(jnp.isfinite(amax), amax, 0.0)
        ex = jnp.exp(alpha - amax[dst])
        denom = jax.ops.segment_sum(ex, dst, num_segments=N)
        w = ex / (denom[dst] + 1e-16)
        out = jax.ops.segment_sum(h[src] * w[:, None], dst, num_segments=N)
        return out + bias

    def _L1_gnn_ref(x, edge_row, edge_col, edge_val, weight, bias):
        import jax, jax.numpy as jnp
        import numpy as np
        N_NODES = 12500
        N_EDGES = 400000
        D_IN = 128
        D_OUT = 128
        support = jnp.dot(x, weight)
        gathered = support[edge_col] * edge_val[:, None]
        output = jax.ops.segment_sum(gathered, edge_row, num_segments=x.shape[0])
        return output + bias

    def _L2_gnn_ref(node_features, edge_index, W_l1, b_l1, W_r1, W_l2, b_l2, W_r2, W_l3, b_l3, W_r3, W_proj):
        import jax, jax.numpy as jnp
        import numpy as np
        N_NODES = 6250
        N_EDGES = 100000
        D_IN, D_HID, D_OUT = (128, 256, 128)

        def _sage_conv(x, src, dst, W_l, b_l, W_r, num_nodes):
            msgs = x[src]
            agg_sum = jax.ops.segment_sum(msgs, dst, num_segments=num_nodes)
            deg = jax.ops.segment_sum(jnp.ones((src.shape[0],), x.dtype), dst, num_segments=num_nodes)
            agg = agg_sum / jnp.maximum(deg, 1.0)[:, None]
            return agg @ W_l.T + b_l + x @ W_r.T
        n = node_features.shape[0]
        src, dst = (edge_index[0], edge_index[1])
        h = jax.nn.relu(_sage_conv(node_features, src, dst, W_l1, b_l1, W_r1, n))
        res = h
        h = jax.nn.relu(_sage_conv(h, src, dst, W_l2, b_l2, W_r2, n) + res)
        res = h @ W_proj.T
        h = _sage_conv(h, src, dst, W_l3, b_l3, W_r3, n) + res
        return h

    def _L3_gnn_ref(x, edge_index, edge_type, W1, root1, b1, W2, root2, b2, W3, root3, b3):
        import jax, jax.numpy as jnp
        import numpy as np
        IN_CH, HID_CH, OUT_CH, NUM_REL = (128, 256, 128, 8)
        N_NODES, N_EDGES = (6250, 100000)

        def _glorot(key, shape):
            fan_in, fan_out = (shape[-2], shape[-1])
            lim = float(np.sqrt(6.0 / (fan_in + fan_out)))
            return jax.random.uniform(key, shape, jnp.float32, -lim, lim)

        def _rgcn_conv(x, src, dst, etype, W, root, b):
            n, d = x.shape
            r = W.shape[0]
            seg = dst.astype(jnp.int32) * r + etype.astype(jnp.int32)
            msg = x[src]
            agg = jax.ops.segment_sum(msg, seg, num_segments=n * r)
            cnt = jax.ops.segment_sum(jnp.ones((msg.shape[0],), x.dtype), seg, num_segments=n * r)
            mean = agg / jnp.maximum(cnt, 1.0)[:, None]
            mean = mean.reshape(n, r, d)
            out = jnp.einsum('nrd,rdo->no', mean, W) + x @ root + b
            return out
        src, dst = (edge_index[0], edge_index[1])
        h = jax.nn.relu(_rgcn_conv(x, src, dst, edge_type, W1, root1, b1))
        h = jax.nn.relu(_rgcn_conv(h, src, dst, edge_type, W2, root2, b2))
        out = _rgcn_conv(h, src, dst, edge_type, W3, root3, b3)
        return out
    edge_index = jnp.stack([src, dst])
    h = jnp.maximum(_layernorm(x, axis=-1), 0.0)
    x = x + _L0_gnn_ref(h, edge_index, edge_attr_32, L0_gnn_W, L0_gnn_W_edge, L0_gnn_att_src, L0_gnn_att_dst, L0_gnn_att_edge, L0_gnn_bias)
    h = jnp.maximum(_layernorm(x, axis=-1), 0.0)
    x = x + _L1_gnn_ref(h, src, dst, edge_weight, L1_gnn_weight, L1_gnn_bias)
    h = jnp.maximum(_layernorm(x, axis=-1), 0.0)
    x = x + _L2_gnn_ref(h, edge_index, L2_gnn_W_l1, L2_gnn_b_l1, L2_gnn_W_r1, L2_gnn_W_l2, L2_gnn_b_l2, L2_gnn_W_r2, L2_gnn_W_l3, L2_gnn_b_l3, L2_gnn_W_r3, L2_gnn_W_proj)
    h = jnp.maximum(_layernorm(x, axis=-1), 0.0)
    x = x + _L3_gnn_ref(h, edge_index, edge_type_8, L3_gnn_W1, L3_gnn_root1, L3_gnn_b1, L3_gnn_W2, L3_gnn_root2, L3_gnn_b2, L3_gnn_W3, L3_gnn_root3, L3_gnn_b3)
    return x

_drawn_inputs = setup_inputs


def setup_inputs(seed=0):
    import zlib

    import numpy as np

    out = dict(_drawn_inputs(seed))
    spreads = {'L0_gnn_bias': (0.0, 0.1),
     'L2_gnn_b_l1': (0.0, 0.1),
     'L2_gnn_b_l2': (0.0, 0.1),
     'L2_gnn_b_l3': (0.0, 0.292),
     'L3_gnn_b1': (0.0, 0.1),
     'L3_gnn_b2': (0.0, 0.1),
     'L3_gnn_b3': (0.0, 0.603)}
    factors = {'L0_gnn_att_dst': 13.011, 'L1_gnn_bias': 2.893}
    for name, (base, spread) in spreads.items():
        noise = np.random.default_rng([zlib.crc32(name.encode()), seed]).standard_normal(out[name].shape)
        drawn = base * np.exp(spread * noise) if base else spread * noise
        out[name] = jnp.asarray(drawn.astype(out[name].dtype))
    for name, factor in factors.items():
        out[name] = (out[name] * factor).astype(out[name].dtype)
    return out
```

```python
from contextlib import ExitStack

import concourse.bass as bass
from concourse import mybir
from concourse.alu_op_type import AluOpType as ALU

F32, I32, BF16 = mybir.dt.float32, mybir.dt.int32, mybir.dt.bfloat16
ACT = mybir.ActivationFunctionType
AX = mybir.AxisListType.X

P = 128
N, D, HID = 5000, 128, 256
EDGES, EDIM, RELS = 80000, 32, 8
T = EDGES // P
RQ, RB = 125, 5
BLOCKS = -(-N // P)
NP = BLOCKS * P
GN = 4 * P
GROUPS = NP // GN
WIN = 32
WIN_SHIFT = 5
TP = 640
LO = 64
HI = NP // LO
AHEAD = 3
BATCH = 16
HALF = 5
NEG = -1.0e30


def build(nc, a, out):
    ctx = ExitStack()
    with ctx:
        def sb(name, shape, dt=F32):
            return ctx.enter_context(nc.sbuf_tensor(name, shape, dt))

        made = {}

        def sem(name):
            if name not in made:
                made[name] = ctx.enter_context(nc.semaphore(name))
            return made[name]

        X = sb("X", [P, NP])
        ACC_A = sb("ACC_A", [P, 2, NP])
        ACC_B = sb("ACC_B", [P, 2, NP])
        MULTI = sb("MULTI", [P, NP])
        SCR = sb("SCR", [P, 6144])
        REL = sb("REL", [P, TP])
        SRC = sb("SRC", [P, TP], I32)
        KEY = sb("KEY", [P, TP], I32)
        TYP = sb("TYP", [P, TP])
        EWT = sb("EWT", [P, TP])
        WGT = sb("WGT", [P, TP])
        BASEF = sb("BASEF", [1, TP])
        BASEK = sb("BASEK", [1, TP // 5 * 8], I32)
        BASE16 = sb("BASE16", [1, TP], I32)
        cur = sb("cur", [P, 2 * HALF], I32)
        ring = sb("ring", [P, 2 * HALF, HID])
        SEL = sb("SEL", [P, 5, WIN])
        TOH = sb("TOH", [P, 5, RELS])
        TOHT = sb("TOHT", [RELS, 5, P])
        ident = sb("ident", [P, P])
        ones = sb("ones", [P, P])
        iotaW = sb("iotaW", [P, WIN])
        iotaK = sb("iotaK", [P, WIN])
        iotaL = sb("iotaL", [P, LO])
        iotaR = sb("iotaR", [P, RELS])
        part = sb("part", [P, 1])
        spare = sb("spare", [P, 1])
        koff = sb("koff", [P, 1])
        spans = sb("spans", [1, 1], I32)
        stats = sb("stats", [P, 8, 6])
        mv8 = sb("mv8", [P, 8, 2])
        mv = sb("mv", [P, BLOCKS, 2])
        std = sb("std", [P, BLOCKS])
        rstd = sb("rstd", [P, BLOCKS])
        shift = sb("shift", [P, BLOCKS])
        small = sb("small", [P, 2 * BATCH])
        W0 = sb("W0", [P, D])
        W1 = sb("W1", [P, D])
        Wl1T = sb("Wl1T", [P, HID])
        Wr1T = sb("Wr1T", [P, HID])
        Wl2T = sb("Wl2T", [P, 2, HID])
        Wr2T = sb("Wr2T", [P, 2, HID])
        Wl3T = sb("Wl3T", [P, 2, D])
        Wr3T = sb("Wr3T", [P, 2, D])
        WpjT = sb("WpjT", [P, 2, D])
        root1 = sb("root1", [P, HID])
        root2 = sb("root2", [P, 2, HID])
        root3 = sb("root3", [P, 2, D])
        brow = sb("brow", [1, 3, D])
        bcol = sb("bcol", [P, 4, 2])
        att = sb("att", [P, 4, D])
        before = sb("before", [P, P])
        watt = sb("watt", [P, 2])
        wdst = sb("wdst", [P, P])
        we_sb = sb("we_sb", [EDIM, D])
        vB = sb("vB", [EDIM, P])
        vrow = sb("vrow", [P, EDIM])
        PS = ctx.enter_context(nc.psum_tensor("PS", [P, 8, 512], F32))

        stage = SCR[:, 0:2048].rearrange("p (u c n) -> p u c n", u=2, c=2)
        stage2 = SCR[:, 2048:4096].rearrange("p (u c n) -> p u c n", u=2, c=2)
        outst = SCR[:, 4096:6144].rearrange("p (u n) -> p u n", u=2)
        wraw = SCR[:, 0:18 * P].rearrange("p (k f) -> p k f", f=P)
        hot_hi = SCR[0:HI, 0:3200].rearrange("p (s e) -> p s e", s=5)
        hi_bc = SCR[:, 3200:4800].bitcast(BF16)[0:HI, :].rearrange("p (s e) -> p s e", s=5)

        flatA = ACC_A[:, :, :].rearrange("p c n -> p (c n)")
        flatB = ACC_B[:, :, :].rearrange("p c n -> p (c n)")

        def row_array(k, dt=F32):
            v = flatA[0:RQ, k * 640:(k + 1) * 640]
            return (v if dt == F32 else v.bitcast(dt)).rearrange("q (b j) -> q b j", b=RB)

        src_r, dst_r, typ_r = (row_array(k, I32) for k in range(3))
        ewt_r, src_f, dst_f, rel_f, typ_f = (row_array(k) for k in range(3, 8))
        hi_i = row_array(8, I32)
        aed_r = row_array(9)
        hi_b = flatA[0:RQ, 6400:6720].bitcast(BF16).rearrange("q (b j) -> q b j", b=RB)
        base_f = flatA[0:RQ, 6720:6725]
        high_f = flatA[0:RQ, 6725:6730]
        span_f = flatA[0:RQ, 6730:6731]
        aflat = flatA[:, 6800:7425]
        ea = [flatB[:, 4000 * u:4000 * (u + 1)] for u in range(2)]
        logit_tab = SCR[0:HI, 5000:5000 + LO]
        asrow = flatA[0:1, 0:NP]
        diag = SCR[:, 5120:6144].rearrange("p (u n) -> p u n", u=2)
        maxB = ACC_B[:, 0, :]
        adstB = ACC_B[:, 1, :]
        maxima = [maxB, ACC_B[:, 1, :], ACC_A[:, 0, :], ACC_A[:, 1, :]]
        src_bc = SCR[:, 0:1280].bitcast(I32).rearrange("p (u e) -> p u e", u=2)
        same = SCR[:, 1280:1920].rearrange("p (s e) -> p s e", s=5)
        spread_t = SCR[0:WIN, 1920:2560].rearrange("p (s e) -> p s e", s=5)
        src_col = SCR[:, 2560:3200]
        twins = SCR[:, 3200:3840].rearrange("p (s e) -> p s e", s=5)
        parts_in = SCR[:, 0:5120].rearrange("p (u r n) -> p u r n", u=2, r=5)
        ASRC, ADST, MAXE, AEDG, SLO, ALPHA = (MULTI[:, k * TP:(k + 1) * TP] for k in range(6))
        lk = MULTI[:, 6 * TP:6 * TP + BATCH * WIN]
        pen = MULTI[:, 6 * TP:6 * TP + 2 * BATCH * WIN].rearrange("p (u n) -> p u n", u=2)
        cnt8 = MULTI[0:RELS, :]
        relw = MULTI[:, 0:4096]

        def dram(name, shape, dt=F32):
            return nc.dram_tensor(name, shape, dt).ap()

        base_d = dram("base_d", (TP,))
        hi_d = dram("hi_d", (EDGES,), BF16)
        aed_d = dram("aed_d", (EDGES,))
        tab = [dram("tab_l0", (NP, D)), dram("tab_l1", (NP, D)), dram("tab_l2a", (NP, D)),
               dram("tab_l2b", (NP, HID)), dram("tab_l2c", (NP, D)), dram("tab_l3a", (NP * RELS, HID)),
               dram("tab_l3b", (NP * RELS, HID)), dram("tab_l3c", (NP * RELS, D))]

        part_d = [dram(f"part_{n}", (NP + P, D)) for n in range(2 * HALF)]

        PASS = [dict(F=D, idx=SRC, wt=WGT, acc=ACC_A, ones=True, zero=True),
                dict(F=D, idx=SRC, wt=EWT, acc=ACC_A, ones=False, zero=True),
                dict(F=D, idx=SRC, wt=None, acc=ACC_A, ones=False, zero=True, count=True),
                dict(F=HID, idx=SRC, wt=None, acc=ACC_A, ones=False, zero=True, lookup=True),
                dict(F=D, idx=SRC, wt=None, acc=ACC_A, ones=False, zero=True),
                dict(F=HID, idx=KEY, wt=WGT, acc=ACC_A, ones=False, zero=False),
                dict(F=HID, idx=KEY, wt=WGT, acc=ACC_B, ones=False, zero=False),
                dict(F=D, idx=KEY, wt=WGT, acc=ACC_A, ones=False, zero=True)]

        def chunks(p):
            return 2 if PASS[p]["F"] == HID or PASS[p]["ones"] else 1

        def rows_of(v):
            return v.rearrange("(b q j) -> q b j", q=RQ, j=P)

        def group_loop(eng, body):
            for u in range(2):
                body(0, u)
            with eng.Fori(1, GROUPS // 2) as i:
                for u in range(2):
                    body(i, u)

        def later(i):
            return not isinstance(i, int) or i > 0

        def cols(v, g, n=GN):
            return v[:, bass.ds(g * n, n)]

        def cols2(v, g):
            return v[:, :, bass.ds(g * GN, GN)]

        class Chain:

            def __init__(self, eng, name, base=0):
                self.eng, self.s, self.n = eng, sem(name), base

            def __call__(self, ins):
                ins.then_inc(self.s, 1)
                self.n = self.n + 1
                self.eng.wait_ge(self.s, self.n)

        def rounds(eng):
            eng.wait_ge(sem("spans_known"), 1)
            return eng.value_load(spans[0:1, 0:1], min_val=1, max_val=NP // WIN + 1)

        def window_regs(eng, who, n=HALF):
            return [eng.alloc_register(name=f"{who}_window{j}") for j in range(n)]

        def windows(eng, regs, first):
            eng.load(regs, first)
            return [eng.snap(r, min_val=0, max_val=NP - WIN) for r in regs]

        def five(q):
            return BASEK[0:1, bass.ds(q * 8, HALF)]

        block = ctx.enter_context(nc.Block())

        FIRST_TABLES = {5: (1, 2, 2048), 6: (2, 2, 2048), 7: (2, 1, 1024)}

        STORED = {0: 0, 1: 1, 2: 2, 4: 3}
        UNITS = {5: 0, 6: 8 * GROUPS, 7: 16 * GROUPS}
        ROUNDS = ["adst", "max", "max_edge"] + [f"p{p}" for p in range(8)]
        X_TERMS = {n: k for k, n in enumerate(("e1", "e2", "e4", "e5", "t7", "e8"))}
        X_PRODUCTS = {n: k for k, n in enumerate(("e1", "e4", "e5", "t7", "e8"))}
        MEANS = {n: k for k, n in enumerate(("e3", "e4", "e5"))}
        PASS_OF = {"e2": 2, "e8": 8}

        def table_ready(p):
            half = 16 * GROUPS // 2
            if p in STORED:
                return [(sem(f"group_stored{u}"), (STORED[p] + 1) * half) for u in range(2)]
            if p == 3:
                return [(sem(f"e3_stored{u}"), 2 * half) for u in range(2)]
            return [(sem(f"unit_stored{u}"), 16 * (UNITS[p] // 2 + GROUPS * 2 * FIRST_TABLES[p][1])) for u in range(2)]

        @block.sync
        def _(sp):
            def load(dst, src, s):
                sp.dma_start(dst, src, allow_slow_non_contiguous=True).then_inc(sem(s), 16)

            for v, name in ((src_r, "src"), (dst_r, "dst"), (typ_r, "edge_type_8"), (ewt_r, "edge_weight")):
                load(v, rows_of(a[name]), "rows_loaded")
            full = N // P
            sp.wait_ge(sem("x_padded"), 1)
            load(X[:, 0:full * P].rearrange("p (b f) -> p b f", f=D),
                 a["x"][0:full * P, :].rearrange("(b p) f -> p b f", p=P), "x_loaded")
            load(X[0:N - full * P, full * P:NP], a["x"][full * P:N, :], "x_loaded")
            for k, name in enumerate(("att_src", "att_dst", "att_edge")):
                load(att[:, k, :], a["L0_gnn_" + name].rearrange("(o f) -> o f", o=1).to_broadcast([P, D]), "w_loaded")
            load(att[:, 3, :], a["L1_gnn_bias"].rearrange("(o f) -> o f", o=1).to_broadcast([P, D]), "w_loaded")
            load(W0[:, :], a["L0_gnn_W"], "w_loaded")
            load(we_sb[:, :], a["L0_gnn_W_edge"], "w_loaded")
            load(W1[:, :], a["L1_gnn_weight"], "w_loaded")
            at = 0
            for name, oc, fc in (("W_l1", 2, 1), ("W_r1", 2, 1), ("W_l2", 2, 2), ("W_r2", 2, 2),
                                 ("W_l3", 1, 2), ("W_r3", 1, 2), ("W_proj", 1, 2)):
                for o in range(oc):
                    load(wraw[:, at:at + fc, :], a["L2_gnn_" + name][o * P:(o + 1) * P, :]
                         .rearrange("o (c f) -> o c f", f=P), "w_loaded")
                    at += fc
            load(root1[:, :], a["L3_gnn_root1"], "w_loaded")
            load(root2[:, :, :], a["L3_gnn_root2"].rearrange("(c p) o -> p c o", p=P), "w_loaded")
            load(root3[:, :, :], a["L3_gnn_root3"].rearrange("(c p) o -> p c o", p=P), "w_loaded")
            for k, name in enumerate(("L0_gnn_bias", "L2_gnn_b_l3", "L3_gnn_b3")):
                load(brow[0:1, k, :], a[name].rearrange("(o f) -> o f", o=1), "w_loaded")
            for k, name in enumerate(("L2_gnn_b_l1", "L2_gnn_b_l2", "L3_gnn_b1", "L3_gnn_b2")):
                load(bcol[:, k, :], a[name].rearrange("(c p) -> p c", p=P), "w_loaded")
            ea_v = a["edge_attr_32"].rearrange("(p c j) f -> c p (j f)", p=P, c=5)
            for c in range(5):
                if c >= 2:
                    sp.wait_ge(sem("ea_used"), c - 1)
                sp.dma_start(ea[c % 2], ea_v[c]).then_inc(sem(f"ea_loaded{c % 2}"), 16)
            sp.wait_ge(sem("zero_made"), 1)
            sp.wait_ge(sem("w_loaded"), 16 * 28)
            for n in range(2 * HALF):
                row = ring[:, 0, 0:D] if n else att[:, 3, :]
                sp.dma_start(part_d[n].rearrange("(p b) f -> p b f", p=P), row.unsqueeze(1).to_broadcast([P, BLOCKS + 1, D])) \
                    .then_inc(sem("parts_zeroed"), 16)
            sp.wait_ge(sem("base_made"), 1)
            load(base_d[0:T].rearrange("(b q) -> q b", q=RQ), base_f, "base_stored")
            sp.wait_ge(sem("base_stored"), 16)
            sp.wait_ge(sem("x_padded"), 2)
            load(BASEF[:, 0:T], base_d[0:T].rearrange("(o t) -> o t", o=1), "base_loaded")
            sp.wait_ge(sem("hi_made"), 1)
            load(rows_of(hi_d), hi_b, "hi_stored")
            sp.wait_ge(sem("aed_made"), 5)
            load(aed_d.rearrange("(p j) -> p j", p=P), aflat, "aed_stored")
            sp.wait_ge(sem("aed_stored"), 16)
            load(aed_r, rows_of(aed_d), "aed_loaded")

            def store_h(k):
                def body(i, u):
                    g = 2 * i + u
                    sp.wait_ge(sem("ln_h"), k * GROUPS + g + 1)
                    sp.dma_start(tab[k][bass.ds(g * GN, GN), :].rearrange("(b p) f -> p b f", p=P),
                                 stage[:, u, 0, :].rearrange("p (b f) -> p b f", f=D)).then_inc(sem(f"group_stored{u}"), 16)
                group_loop(sp, body)

            store_h(0)
            sp.wait_ge(sem("asrow_done"), GROUPS)
            load(logit_tab, asrow.rearrange("o (h l) -> o h l", l=LO), "logits_loaded")
            sp.wait_ge(sem("hi_stored"), 16)
            sp.wait_ge(sem("ln0_mm"), GROUPS)
            for u in range(2):
                sp.wait_ge(sem(f"group_stored{u}"), 16 * GROUPS // 2)

            def hi_chunk(i, s):
                src = hi_d[bass.ds((5 * i + s) * 640, 640)].rearrange("(o e) -> o e", o=1).to_broadcast([HI, 640])
                sp.dma_start(hi_bc[:, s, :], src).then_inc(sem(f"hi_loaded{s}"), 16)
            for s in range(5):
                hi_chunk(0, s)
            with sp.Fori(1, 25) as i:
                for s in range(5):
                    sp.wait_ge(sem("hot_made"), 5 * i + s - 4)
                    hi_chunk(i, s)

            def support(i, u):
                g = 2 * i + u
                sp.wait_ge(sem("e1_out"), g + 1)
                sp.dma_start(tab[1][bass.ds(g * GN, GN), :].rearrange("(b p) f -> p b f", p=P),
                             outst[:, u, 0:GN].rearrange("p (b f) -> p b f", f=D)).then_inc(sem(f"group_stored{u}"), 16)
            group_loop(sp, support)
            km = rounds(sp)
            regs = window_regs(sp, "sp")
            for u in range(2):
                sp.wait_ge(sem(f"group_stored{u}"), 2 * 16 * GROUPS // 2)
            sp.wait_ge(sem("src_col"), 1)
            with sp.Fori(0, km) as k:
                sp.wait_ge(sem("round"), (km * 3 + 1) * ROUNDS.index("p1") + k * 3 + 4)
                sp.sem_inc(sem("sp_turn"), 1)
                kk = sp.snap(km + k)

                def half(q, h, done, sources_used):
                    first = windows(sp, regs, five(q))
                    if sources_used is not None:
                        sp.wait_ge(sem("idx_ready"), sources_used)
                        sp.sem_inc(sem("sp_turn"), 1)
                    src = a["src"][bass.ds(q * HALF * P, HALF * P)].rearrange("(o e) -> o e", o=1).to_broadcast([P, HALF * P])
                    sp.dma_start(src_bc[:, h, :], src).then_inc(sem(f"src_bc{h}"), 16)
                    sp.wait_ge(sem("mm_done"), done)
                    sp.sem_inc(sem("sp_turn"), 1)
                    for j in range(HALF):
                        s = h * HALF + j
                        sp.dma_start(ring[0:WIN, s, D:2 * D], tab[1][bass.ds(first[j], WIN), :]).then_inc(sem(f"window{h}"), 16)
                half(0, 0, kk * T + 1, None)
                half(1, 1, kk * T + 1, None)
                with sp.Fori(1, T // (2 * HALF)) as r:
                    for h in range(2):
                        q = 2 * r + h
                        half(q, h, kk * T + (q - 1) * HALF + 1, kk * (T // HALF) + q - 1)
                half(T // HALF - 1, 0, (kk + 1) * T - 2 * HALF + 1, (kk + 1) * (T // HALF) - 2)
                sp.wait_ge(sem("idx_ready"), (kk + 1) * (T // HALF))
                sp.sem_inc(sem("sp_turn"), 1)
            sp.wait_ge(sem("scat0"), km * (80 * 63))
            sp.sem_inc(sem("sp_turn"), 1)
            sp.wait_ge(sem("scat1"), km * (80 * 62))
            sp.sem_inc(sem("sp_turn"), 1)

            def parts(i, u):
                if later(i):
                    sp.wait_ge(sem("x_added"), X_TERMS["e2"] * GROUPS + i)
                    sp.sem_inc(sem("sp_turn"), 1)
                for n in range(HALF):
                    sp.dma_start(parts_in[:, u, n, :].rearrange("p (b f) -> p b f", f=D),
                                 part_d[u * HALF + n][bass.ds(i * GN, GN), :].rearrange("(b p) f -> p b f", p=P)).then_inc(sem(f"parts_in{u}"), 16)
            for u in range(2):
                parts(0, u)
            with sp.Fori(1, GROUPS) as i:
                for u in range(2):
                    parts(i, u)
            store_h(2)
            def e3(i, u):
                g = 2 * i + u
                for j in range(2):
                    sp.wait_ge(sem("e3_out"), 2 * g + j + 1)
                    sp.dma_start(tab[3][bass.ds(g * GN + 2 * j * P, 2 * P), :].rearrange("(b p) f -> p b f", p=P),
                                 outst[:, j, 0:512].rearrange("p (b f) -> p b f", f=HID)).then_inc(sem(f"e3_stored{j}"), 16)
            group_loop(sp, e3)
            def e4(i, u):
                g = 2 * i + u
                sp.wait_ge(sem("e4_out"), g + 1)
                sp.dma_start(tab[4][bass.ds(g * GN, GN), :].rearrange("(b p) f -> p b f", p=P),
                             outst[:, u, 0:GN].rearrange("p (b f) -> p b f", f=D)).then_inc(sem(f"group_stored{u}"), 16)
            group_loop(sp, e4)

            def relation_table(p, weight):
                kc, halves, width = FIRST_TABLES[p]
                for c in range(kc):
                    load(relw[:, c * width:(c + 1) * width].rearrange("p (r o) -> p r o", r=RELS),
                         weight[:, c * P:(c + 1) * P, :].rearrange("r f o -> f r o"), "relw_loaded")
                rows = tab[p].rearrange("(n h) f -> n (h f)", n=NP)

                def body(i, u):
                    g = 2 * i + u
                    per = 4 * halves
                    for j in range(per):
                        sp.wait_ge(sem("unit_outa"), UNITS[p] + g * per + j + 1)
                        sp.wait_ge(sem("unit_outd"), UNITS[p] + g * per + j + 1)
                        b, h = j // halves, j % halves
                        sp.dma_start(rows[bass.ds(g * GN + b * P, P), h * 1024:(h + 1) * 1024],
                                     outst[:, j % 2, :]).then_inc(sem(f"unit_stored{j % 2}"), 16)
                group_loop(sp, body)

            sp.wait_ge(sem("x_added"), X_TERMS["e5"] * GROUPS + GROUPS)
            relation_table(5, a["L3_gnn_W1"])
            relation_table(6, a["L3_gnn_W2"])
            relation_table(7, a["L3_gnn_W3"])
            sp.wait_ge(sem("x_final"), 1)
            sp.dma_start(out[0:full * P, :].rearrange("(b p) f -> p b f", p=P),
                         X[:, 0:full * P].rearrange("p (b f) -> p b f", f=D)).then_inc(sem("stored"), 16)
            sp.dma_start(out[full * P:N, :], X[0:N - full * P, full * P:NP]).then_inc(sem("stored"), 16)
            sp.wait_ge(sem("stored"), 32)

        @block.gpsimd
        def _(pool):
            pool.memset(X[:, (BLOCKS - 1) * P:NP], 0.0).then_inc(sem("x_padded"), 1)
            pool.memset(BASEF[:, :], 0.0).then_inc(sem("x_padded"), 1)
            pool.memset(ident[:, :], 0.0).then_inc(sem("ident0"), 1)
            spare_rows = spare[:, :]
            for v, pat, mul in ((iotaW[:, :], [[1, WIN]], 0), (iotaL[:, :], [[1, LO]], 0),
                                (iotaR[:, :], [[1, RELS]], 0), (part[:, :], [[0, 1]], 1), (spare_rows, [[0, 1]], 1)):
                pool.iota(v, pat, base=NP if v is spare_rows else 0, channel_multiplier=mul, allow_small_or_imprecise_dtypes=True).then_inc(sem("const"), 1)
            pool.memset(ones[:, :], 1.0).then_inc(sem("const"), 1)
            pool.memset(ring[:, 0, 0:D], 0.0).then_inc(sem("zero_made"), 1)
            pool.memset(before[:, :], 0.0).then_inc(sem("ident0"), 1)
            pool.wait_ge(sem("ident0"), 2)
            pool.affine_select(out=before[:, :], in_=before[:, :], compare_op=ALU.is_ge, fill=1.0, base=0,
                               pattern=[[1, P]], channel_multiplier=-1).then_inc(sem("const"), 1)
            pool.affine_select(out=ident[:, :], in_=ident[:, :], compare_op=ALU.not_equal, fill=1.0, base=0,
                               pattern=[[-1, P]], channel_multiplier=1).then_inc(sem("const"), 1)

            def hot(i, s):
                pool.wait_ge(sem(f"hi_loaded{s}"), 16 * (i + 1))
                if later(i):
                    pool.sem_inc(sem("gather_turn"), 1)
                    pool.wait_ge(sem("src_mm"), 5 * i + s - 4)
                    pool.sem_inc(sem("gather_turn"), 1)
                pool.tensor_scalar(hot_hi[:, s, :], hi_bc[:, s, :], part[0:HI, :], None, ALU.is_equal).then_inc(sem("hot_made"), 1)
            pool.wait_ge(sem("const"), 8)
            for s in range(5):
                hot(0, s)
            with pool.Fori(1, 25) as i:
                for s in range(5):
                    hot(i, s)
            km = rounds(pool)

            def gather(p):
                width = PASS[p]["F"]
                for s, n in table_ready(p):
                    pool.wait_ge(s, n)
                with pool.Fori(0, km) as k:
                    kk = pool.snap(km * p + k)

                    def half(q, h):
                        pool.wait_ge(sem("idx_ready"), kk * (T // HALF) + q + 1)
                        pool.sem_inc(sem("gather_turn"), 1)
                        for j in range(HALF):
                            s = h * HALF + j
                            pool.indirect_dma_start(ring[:, s, 0:width], None, tab[p][:, :],
                                                    bass.IndirectOffsetOnAxis(cur[:, s:s + 1], 0)).then_inc(sem(f"row{s}"), 16)
                    with pool.Fori(0, T // (2 * HALF)) as r:
                        for h in range(2):
                            half(2 * r + h, h)
                    half(T // HALF - 1, 0)

            def scatter():
                with pool.Fori(0, km) as k:
                    kk = pool.snap(km + k)

                    def half(q, h):
                        pool.wait_ge(sem("idx_ready"), kk * (T // HALF) + q + 1)
                        pool.sem_inc(sem("gather_turn"), 1)
                        pool.wait_ge(sem("psum_free"), kk * T + (q + 1) * HALF + 5)
                        pool.sem_inc(sem("gather_turn"), 1)
                        for j in range(HALF):
                            s = h * HALF + j
                            pool.indirect_dma_start(part_d[s][:, :], bass.IndirectOffsetOnAxis(cur[:, s:s + 1], 0), ring[:, s, 0:D], None,
                                                    compute_op=ALU.add).then_inc(sem(f"scat{h}"), 16)
                    with pool.Fori(0, T // (2 * HALF)) as r:
                        for h in range(2):
                            half(2 * r + h, h)
                    half(T // HALF - 1, 0)

            pool.wait_ge(sem("parts_zeroed"), 16 * 2 * HALF)
            for p in range(len(PASS)):
                scatter() if p == 1 else gather(p)

        @block.scalar
        def _(act):
            act.wait_ge(sem("watt_made"), 3)
            nc.scalar.copy(wdst[:, :], watt[:, 1:2].to_broadcast([P, P])).then_inc(sem("wdst_made"), 1)
            nc.scalar.copy(vB[:, :], small[0:EDIM, 0:1].to_broadcast([EDIM, P])).then_inc(sem("vB_made"), 1)

            def norm_start(k):
                act.wait_ge(sem("ln_var"), k + 1)
                nc.scalar.activation(std[:, :], std[:, :], ACT.Sqrt).then_inc(sem("ln_std"), 1)
                act.wait_ge(sem("ln_shift"), k + 1)

            def norm_group(k, i, u):
                g = 2 * i + u
                if later(i):
                    if k in (0, 2):
                        act.wait_ge(sem(f"group_stored{u}"), 16 * (STORED[k] * GROUPS // 2 + i))
                    act.wait_ge(sem("ln_tr"), k * GROUPS + g - 1)
                for q in range(4):
                    ins = nc.scalar.activation(stage[:, u, 0, q * P:(q + 1) * P], cols(X, 4 * g + q, P), ACT.Relu,
                                               bias=cols(shift, 4 * g + q, 1), scale=cols(rstd, 4 * g + q, 1))
                ins.then_inc(sem("ln_h"), 1)

            def indices(p):
                idx = PASS[p]["idx"]
                with act.Fori(0, km) as k:
                    kk = act.snap(km * p + k)

                    def half(q, h, done):
                        act.wait_ge(sem("mm_done"), kk * T + done + 1)
                        nc.scalar.copy(cur[:, h * HALF:(h + 1) * HALF], cols(idx, q, HALF)).then_inc(sem("idx_ready"), 1)

                    def onehots(q):
                        if PASS[p].get("lookup"):
                            for j in range(HALF):
                                act.wait_ge(sem("toh_tr"), k * T + q * HALF + j + 1)
                                nc.scalar.copy(TOHT[:, j, :], PS[0:RELS, j, P:2 * P]).then_inc(sem("toht_made"), 1)
                    half(0, 0, 0)
                    half(1, 1, 0)
                    onehots(0)
                    with act.Fori(1, T // (2 * HALF)) as r:
                        for h in range(2):
                            half(2 * r + h, h, (2 * r + h - 1) * HALF)
                            onehots(2 * r + h - 1)
                    half(T // HALF - 1, 0, T - 2 * HALF)
                    onehots(T // HALF - 2)
                    onehots(T // HALF - 1)

            def bias_rows(name, dst, bank_of, b, i, u):
                g = 2 * i + u
                act.wait_ge(sem(name + "_root"), g + 1)
                for o in range(2):
                    ins = nc.scalar.activation(dst[:, o, bass.ds(g * GN, GN)], PS[:, bank_of(o), :], ACT.Identity,
                                               bias=bcol[:, b, o:o + 1])
                ins.then_inc(sem(name + "_rooted"), 1)

            def unit_out(p, i, u, j):
                per = 4 * FIRST_TABLES[p][1]
                g = 2 * i + u
                act.wait_ge(sem("unit"), UNITS[p] + g * per + j + 1)
                if later(i) or u or j >= 2:
                    act.wait_ge(sem(f"unit_stored{j % 2}"), 16 * (UNITS[p] // 2 + g * (per // 2) + j // 2))
                nc.scalar.copy(outst[:, j % 2, 0:512], PS[:, 2 * (j % 2), :]).then_inc(sem("unit_outa"), 1)

            def l0(i, u):
                g = 2 * i + u
                norm_group(0, i, u)
                act.wait_ge(sem("ln0_mm"), g + 1)
                nc.scalar.copy(asrow[:, bass.ds(g * GN, GN)], PS[0:1, u, :]).then_inc(sem("asrow_done"), 1)
            act.wait_ge(sem("cols_done"), 10)
            act.wait_ge(sem("wT_done"), 7)
            norm_start(0)
            group_loop(act, l0)
            km = rounds(act)
            with act.Fori(0, km) as k:
                def spread(g, s):
                    n = k * (TP // BATCH) + g
                    act.wait_ge(sem("mx_red"), n + 1)
                    act.sem_inc(sem("act_turn"), 1)
                    for q in range(4):
                        ins = nc.scalar.mul(diag[:, s, q * P:(q + 1) * P], ident[:, :], small[:, 4 + 4 * s + q:5 + 4 * s + q])
                    ins.then_inc(sem("mx_diag"), 1)
                with act.Fori(0, TP // BATCH // 2) as i:
                    for s in range(2):
                        spread(2 * i + s, s)
            act.wait_ge(sem("exp_in"), 1)
            nc.scalar.activation(WGT[:, :], WGT[:, :], ACT.Exp).then_inc(sem("wgt_made"), 1)
            act.sem_inc(sem("mm_done"), 1)
            indices(0)
            norm_start(1)

            def l1(i, u):
                norm_group(1, i, u)
                act.wait_ge(sem("e1_tab"), 2 * i + u + 1)
                if later(i):
                    act.wait_ge(sem(f"group_stored{u}"), 16 * (STORED[1] * GROUPS // 2 + i))
                nc.scalar.copy(outst[:, u, 0:512], PS[:, 2 + u, :]).then_inc(sem("e1_out"), 1)
            group_loop(act, l1)
            with act.Fori(0, km) as k:
                kk = act.snap(km + k)

                def spread_copy(t, s):
                    act.wait_ge(sem("b_mm"), k * T + t + 1)
                    nc.scalar.copy(spread_t[:, s, :], PS[0:WIN, s, 0:P]).then_inc(sem("b_ready"), 1)

                def rows_copy(t, slot):
                    act.wait_ge(sem("mm_done"), kk * T + t + 2)
                    nc.scalar.copy(ring[:, slot, 0:D], PS[:, slot % 5, P:2 * P]).then_inc(sem("psum_free"), 1)

                def half(q, h, landed, last=False):
                    if landed is not None:
                        act.wait_ge(sem(f"scat{h}"), landed)
                    for j in range(HALF):
                        if not (last and j == HALF - 1):
                            spread_copy(q * HALF + j + 1, (j + 1) % 5)
                        rows_copy(q * HALF + j, h * HALF + j)
                spread_copy(0, 0)
                half(0, 0, None)
                half(1, 1, None)
                with act.Fori(1, T // (2 * HALF)) as r:
                    for h in range(2):
                        half(2 * r + h, h, (k * (T // 10 + (h == 0)) + r) * 80)
                half(T // HALF - 1, 0, (k * (T // 10 + 1) + T // 10) * 80, True)
                act.wait_ge(sem("scat0"), (k + 1) * (80 * 63))
                act.wait_ge(sem("scat1"), (k + 1) * (80 * 62))
                act.sem_inc(sem("act_turn"), 1)
            norm_start(2)

            def l2(i, u):
                norm_group(2, i, u)
                bias_rows("ln2", ACC_B, lambda o: 2 * u + o, 0, i, u)
            group_loop(act, l2)
            indices(2)
            def e3(i, u):
                g = 2 * i + u
                act.wait_ge(sem("e3_pre"), g + 1)
                nc.scalar.activation(stage2[:, u, :, :], stage2[:, u, :, :], ACT.Relu).then_inc(sem("e3_hid"), 1)
                for j in range(2):
                    act.wait_ge(sem("e3_tr"), 2 * g + j + 1)
                    if later(i) or u:
                        act.wait_ge(sem(f"e3_stored{j}"), 16 * g)
                    nc.scalar.copy(outst[:, j, 0:512], PS[:, 5 + j, :]).then_inc(sem("e3_out"), 1)
            group_loop(act, e3)
            indices(3)
            def e4(i, u):
                g = 2 * i + u
                act.wait_ge(sem("e4_pre"), g + 1)
                nc.scalar.activation(stage2[:, u, :, :], stage2[:, u, :, :], ACT.Relu).then_inc(sem("e4_hid"), 1)
                act.wait_ge(sem("e4_tab"), g + 1)
                if later(i):
                    act.wait_ge(sem(f"group_stored{u}"), 16 * (STORED[4] * GROUPS // 2 + i))
                nc.scalar.copy(outst[:, u, 0:512], PS[:, 5, :]).then_inc(sem("e4_out"), 1)
            group_loop(act, e4)
            indices(4)
            norm_start(3)

            def t5(i, u):
                norm_group(3, i, u)
                bias_rows("t5", ACC_A, lambda o: 4 + 3 * o, 2, i, u)
                for j in range(8):
                    unit_out(5, i, u, j)
            group_loop(act, t5)
            indices(5)

            def hidden_group(p, acc, i, u):
                g = 2 * i + u
                act.wait_ge(sem("pass_end"), p)
                if later(i):
                    act.wait_ge(sem("unit"), UNITS[p] + (g - 1) * 4 * FIRST_TABLES[p][1])
                    if p == 7:
                        act.wait_ge(sem("x_mm"), X_PRODUCTS["t7"] * GROUPS + g - 1)
                    else:
                        act.wait_ge(sem(f"t{p}_root"), g - 1)
                nc.scalar.activation(stage2[:, u, :, :], cols2(acc, g), ACT.Relu).then_inc(sem(f"t{p}_hid"), 1)

            def t6(i, u):
                hidden_group(6, ACC_A, i, u)
                bias_rows("t6", ACC_B, lambda o: 4 + 3 * o, 3, i, u)
                for j in range(8):
                    unit_out(6, i, u, j)
            group_loop(act, t6)
            indices(6)
            def t7(i, u):
                hidden_group(7, ACC_B, i, u)
                for j in range(4):
                    unit_out(7, i, u, j)
            group_loop(act, t7)
            indices(7)
            def copy_sums(name, i, u):
                g = 2 * i + u
                if later(i):
                    act.wait_ge(sem("x_mm"), X_PRODUCTS[name] * GROUPS + g - 1)
                act.wait_ge(sem("pass_end"), PASS_OF[name])
                nc.scalar.copy(stage[:, u, 0, :], cols(ACC_A[:, 0, :], g)).then_inc(sem(name + "_stage"), 1)
            group_loop(act, lambda i, u: copy_sums("e8", i, u))


        @block.vector
        def _(dve):
            vec = nc.vector
            link = Chain(dve, "dve_step")

            dve.wait_ge(sem("const"), 8)
            vec.memset(REL[:, :], -1.0).then_inc(sem("cleared"), 1)
            vec.memset(TYP[:, :], 0.0).then_inc(sem("cleared"), 1)
            vec.memset(EWT[:, :], 0.0).then_inc(sem("cleared"), 1)
            vec.memset(MULTI[:, 0:6 * TP], 0.0).then_inc(sem("cleared"), 1)
            dve.wait_ge(sem("rows_loaded"), 64)
            vec.tensor_copy(dst_f, dst_r).then_inc(sem("dst_f"), 1)
            vec.tensor_copy(src_f, src_r).then_inc(sem("rows_made"), 1)
            vec.tensor_copy(typ_f, typ_r).then_inc(sem("rows_made"), 1)
            link(vec.tensor_scalar(hi_i, src_r, LO.bit_length() - 1, None, ALU.arith_shift_right))
            vec.tensor_copy(hi_b, hi_i).then_inc(sem("hi_made"), 1)
            dve.wait_ge(sem("dst_f"), 1)
            vec.tensor_reduce(high_f, dst_f, AX, ALU.max).then_inc(sem("dst_f"), 1)
            vec.tensor_reduce(base_f, dst_f, AX, ALU.min).then_inc(sem("base_made"), 1)
            dve.wait_ge(sem("base_made"), 1)
            dve.wait_ge(sem("dst_f"), 2)
            vec.tensor_tensor(rel_f, dst_f, base_f.unsqueeze(2).to_broadcast([RQ, RB, P]), ALU.subtract).then_inc(sem("rows_made"), 1)
            link(vec.tensor_tensor(high_f, high_f, base_f, ALU.subtract))
            vec.tensor_reduce(span_f, high_f, AX, ALU.max).then_inc(sem("rows_made"), 1)
            dve.wait_ge(sem("cleared"), 4)
            for n, v in enumerate((SRC, TYP, REL, EWT)):
                dve.wait_ge(sem("rows_tr"), n + 1)
                vec.tensor_copy(v[:, 0:500], PS[:, 2 * n, 0:500]).then_inc(sem("cols_done"), 1)
                vec.tensor_copy(v[:, 500:T], PS[:, 2 * n + 1, 0:T - 500]).then_inc(sem("cols_done"), 1)
            dve.wait_ge(sem("cols_done"), 8)
            vec.scalar_tensor_tensor(KEY[:, 0:500], PS[:, 0, 0:500], float(RELS), TYP[:, 0:500], ALU.mult, ALU.add).then_inc(sem("cols_done"), 1)
            vec.scalar_tensor_tensor(KEY[:, 500:T], PS[:, 1, 0:T - 500], float(RELS), TYP[:, 500:T], ALU.mult, ALU.add).then_inc(sem("cols_done"), 1)
            low = ALPHA.bitcast(I32)[:, 0:T]
            link(vec.tensor_scalar(low, SRC[:, 0:T], LO - 1, None, ALU.bitwise_and))
            link(vec.tensor_copy(SLO[:, 0:T], low))
            link(vec.memset(ALPHA, 0.0))

            dve.wait_ge(sem("w_loaded"), 16 * 28)
            junk = outst[:, 0, 0:D]
            link(vec.scalar_tensor_tensor(junk, W0[:, :], 1.0, att[:, 0, :], ALU.mult, ALU.mult, accum_out=watt[:, 0:1]))
            dve.sem_inc(sem("watt_made"), 1)
            link(vec.scalar_tensor_tensor(junk, W0[:, :], 1.0, att[:, 1, :], ALU.mult, ALU.mult, accum_out=watt[:, 1:2]))
            dve.sem_inc(sem("watt_made"), 1)
            link(vec.scalar_tensor_tensor(junk[0:EDIM, :], we_sb[:, :], 1.0, att[0:EDIM, 2, :], ALU.mult, ALU.mult, accum_out=small[0:EDIM, 0:1]))
            dve.sem_inc(sem("watt_made"), 1)
            dve.wait_ge(sem("wT_tr"), 1)
            at = 0
            for w, oc, fc in ((Wl1T, 2, 1), (Wr1T, 2, 1), (Wl2T, 2, 2), (Wr2T, 2, 2), (Wl3T, 1, 2), (Wr3T, 1, 2), (WpjT, 1, 2)):
                for o in range(oc):
                    for c in range(fc):
                        dst = w[:, o * P:(o + 1) * P] if fc == 1 else w[:, c, o * P:(o + 1) * P]
                        ins = vec.tensor_copy(dst, PS[:, at // 4, (at % 4) * P:(at % 4 + 1) * P])
                        at += 1
                ins.then_inc(sem("wT_done"), 1)
            dve.wait_ge(sem("span_tr"), 1)
            link(vec.tensor_reduce(small[0:1, 2:3], PS[0:1, 5, 0:RQ], AX, ALU.max))
            link(vec.tensor_copy(spans[:, :], small[0:1, 2:3]))
            link(vec.tensor_scalar(spans[:, :], spans[:, :], WIN_SHIFT, None, ALU.arith_shift_right))
            link(vec.tensor_scalar(spans[:, :], spans[:, :], 1.0, None, ALU.add))
            dve.sem_inc(sem("spans_known"), 5)

            dve.wait_ge(sem("vrow_mm"), 1)
            link(vec.tensor_copy(vrow[:, :], PS[:, 6, 0:EDIM]))
            for c in range(5):
                v = ea[c % 2].rearrange("p (j f) -> p j f", f=EDIM)
                dve.wait_ge(sem(f"ea_loaded{c % 2}"), 16 * (c // 2 + 1))
                link(vec.tensor_tensor(v, v, vrow[:, :].unsqueeze(1).to_broadcast([P, 125, EDIM]), ALU.mult))
                link(vec.tensor_reduce(aflat[:, c * 125:(c + 1) * 125], v, AX, ALU.add))
                dve.sem_inc(sem("ea_used"), 1)
                dve.sem_inc(sem("aed_made"), 1)

            def norm_stats(k):
                c, n = sem("ln_stats"), 3 * BLOCKS // 8 * k

                def eight(i):
                    if k or later(i):
                        dve.wait_ge(c, n + 3 * i)
                    for j in range(8):
                        ins = vec.bn_stats(stats[:, j, :], cols(X, 8 * i + j, P))
                    ins.then_inc(c, 1)
                    dve.wait_ge(c, n + 3 * i + 1)
                    dve.sem_inc(sem("dve_turn"), 1)
                    for j in range(8):
                        ins = vec.bn_aggr(mv8[:, j, :], stats[:, j, :])
                    ins.then_inc(c, 1)
                    dve.wait_ge(c, n + 3 * i + 2)
                    vec.tensor_copy(mv[:, bass.ds(8 * i, 8), :], mv8[:, :, :]).then_inc(c, 1)
                eight(0)
                with dve.Fori(1, BLOCKS // 8) as i:
                    eight(i)
                dve.wait_ge(c, n + 3 * BLOCKS // 8)
                vec.tensor_scalar(std[:, :], mv[:, :, 1], 1e-5, None, ALU.add).then_inc(sem("ln_var"), 1)
                dve.wait_ge(sem("ln_std"), k + 1)
                link(vec.reciprocal(rstd[:, :], std[:, :]))
                vec.scalar_tensor_tensor(shift[:, :], mv[:, :, 0], -1.0, rstd[:, :], ALU.mult, ALU.mult).then_inc(sem("ln_shift"), 1)

            def transposed_group(k, i, u, used, per):
                g = 2 * i + u
                dve.wait_ge(sem("ln_tr"), k * GROUPS + g + 1)
                if later(i):
                    dve.wait_ge(sem(used), (g - 1) * per)
                vec.tensor_copy(stage2[:, u, 0, :], PS[:, 5 + u, :]).then_inc(sem("ln_ht"), 1)

            def round_start(tag, k):
                s, n = sem("round"), (km * 3 + 1) * ROUNDS.index(tag) + k * 3
                dve.wait_ge(s, n + 1)
                vec.tensor_scalar(iotaK[:, :], iotaW[:, :], koff[:, :], None, ALU.add).then_inc(s, 1)
                if tag in ("adst", "max", "max_edge"):
                    to, bases = BASE16[:, :], BASEF[:, :]
                else:
                    to = BASEK[:, :].rearrange("o (q e) -> o q e", e=8)[:, :, 0:HALF]
                    bases = BASEF[:, :].rearrange("o (q e) -> o q e", e=HALF)
                vec.tensor_scalar(to, bases, koff[0:1, :], float(NP - WIN), ALU.add, ALU.min).then_inc(s, 1)
                dve.wait_ge(s, n + 3)
                vec.tensor_scalar(koff[:, :], koff[:, :], float(WIN), None, ALU.add).then_inc(s, 1)
                dve.wait_ge(s, n + 4)
                dve.sem_inc(sem("dve_turn"), 1)

            def rounds_reset(tag):
                vec.memset(koff[:, :], 0.0).then_inc(sem("round"), 1)

            regs = window_regs(dve, "dve", BATCH)

            dve.wait_ge(sem("x_loaded"), 32)
            dve.wait_ge(sem("x_padded"), 1)
            norm_stats(0)

            def l0(i, u):
                g = 2 * i + u
                transposed_group(0, i, u, "ln0_mm", 1)
                dve.wait_ge(sem("ln0_mm"), g + 1)
                vec.tensor_copy(cols(adstB, g), PS[:, 2 + u, :]).then_inc(sem("adst_done"), 1)
            group_loop(dve, l0)
            dve.wait_ge(sem("aed_tr"), 1)
            link(vec.tensor_copy(AEDG[:, 0:500], PS[:, 5, 0:500]))
            link(vec.tensor_copy(AEDG[:, 500:T], PS[:, 6, 0:T - 500]))

            def pick(q, s):
                v = lk[:, 0:HALF * LO].rearrange("p (j l) -> p j l", l=LO)
                c = sem("pick")
                if later(q):
                    dve.wait_ge(sem("picked"), q)
                vec.tensor_tensor(v, iotaL[:, :].unsqueeze(1).to_broadcast([P, 5, LO]),
                                  cols(SLO, q, 5).unsqueeze(2).to_broadcast([P, 5, LO]), ALU.is_equal).then_inc(c, 1)
                dve.wait_ge(c, q * 2 + 1)
                dve.wait_ge(sem("src_mm"), q + 1)
                vec.tensor_tensor(v, v, PS[:, s, 0:320].rearrange("p (j l) -> p j l", l=LO), ALU.mult).then_inc(c, 1)
                dve.wait_ge(c, q * 2 + 2)
                vec.tensor_reduce(cols(ASRC, q, 5), v, AX, ALU.add).then_inc(sem("picked"), 1)
            for s in range(5):
                pick(s, s)
            with dve.Fori(1, 25) as i:
                for s in range(5):
                    pick(5 * i + s, s)
            km = rounds(dve)
            dve.wait_ge(sem("base_loaded"), 16)

            def lookup(tag, table, dest):
                rounds_reset(tag)
                c = sem("step_" + tag)
                v, found = lk.rearrange("p (j w) -> p j w", w=WIN), small[:, BATCH:2 * BATCH]
                with dve.Fori(0, km) as k:
                    round_start(tag, k)
                    with dve.Fori(0, TP // BATCH) as q:
                        n = dve.snap((k * (TP // BATCH) + q) * 4)
                        first = windows(dve, regs, BASE16[0:1, bass.ds(q * BATCH, BATCH)])
                        vec.tensor_tensor(v, iotaK[:, :].unsqueeze(1).to_broadcast([P, BATCH, WIN]),
                                          cols(REL, q, BATCH).unsqueeze(2).to_broadcast([P, BATCH, WIN]), ALU.is_equal).then_inc(c, 1)
                        dve.wait_ge(c, n + 1)
                        for j in range(BATCH):
                            ins = vec.tensor_tensor(v[:, j, :], v[:, j, :], table[:, bass.ds(first[j], WIN)], ALU.mult)
                        ins.then_inc(c, 1)
                        dve.wait_ge(c, n + 2)
                        vec.tensor_reduce(found, v, AX, ALU.add).then_inc(c, 1)
                        dve.wait_ge(c, n + 3)
                        vec.tensor_tensor(cols(dest, q, BATCH), cols(dest, q, BATCH), found, ALU.add).then_inc(c, 1)
                dve.wait_ge(c, km * (4 * (TP // BATCH)))
                dve.sem_inc(sem("dve_turn"), 1)

            lookup("adst", adstB, ADST)
            dve.wait_ge(sem("picked"), T // 5)
            link(vec.tensor_tensor(ALPHA, ASRC, ADST, ALU.add))
            link(vec.tensor_tensor(ALPHA, ALPHA, AEDG, ALU.add))
            link(vec.scalar_tensor_tensor(ALPHA, ALPHA, 0.2, ALPHA, ALU.mult, ALU.max))

            rounds_reset("max")
            for v in maxima:
                vec.memset(v, NEG).then_inc(sem("mx_done"), 1)
            with dve.Fori(0, km) as k:
                round_start("max", k)

                def masked(g, s):
                    n = k * (TP // BATCH) + g
                    v = pen[:, s, :].rearrange("p (j w) -> p j w", w=WIN)
                    vec.tensor_tensor(v, iotaK[:, :].unsqueeze(1).to_broadcast([P, BATCH, WIN]),
                                      cols(REL, g, BATCH).unsqueeze(2).to_broadcast([P, BATCH, WIN]), ALU.not_equal).then_inc(sem("mx_pen"), 1)
                    dve.wait_ge(sem("mx_pen"), n + 1)
                    vec.scalar_tensor_tensor(v, v, NEG, cols(ALPHA, g, BATCH).unsqueeze(2).to_broadcast([P, BATCH, WIN]),
                                             ALU.mult, ALU.add).then_inc(sem("mx_masked"), 1)

                def reduced(g, s):
                    dve.wait_ge(sem("mx_tr"), k * (TP // BATCH) + g + 1)
                    vec.tensor_reduce(small[:, 4 + 4 * s:8 + 4 * s], PS[:, s, :].rearrange("p (a e) -> p a e", e=P), AX, ALU.max).then_inc(sem("mx_red"), 1)

                def merged(g, s):
                    n = k * (TP // BATCH) + g
                    first = windows(dve, regs, BASE16[0:1, bass.ds(BATCH * g, BATCH)])
                    dve.wait_ge(sem("mx_all"), n + 1)
                    for j in range(BATCH):
                        v = maxima[j % 4][:, bass.ds(first[j], WIN)]
                        if j % 4 == 0:
                            dve.wait_ge(sem("mx_done"), n * (BATCH // 4) + j // 4 + 4)
                        ins = vec.tensor_tensor(v, v, PS[:, 2 + s, j * WIN:(j + 1) * WIN], ALU.max)
                        if j % 4 == 3:
                            ins.then_inc(sem("mx_done"), 1)
                masked(0, 0)
                masked(1, 1)
                reduced(0, 0)
                with dve.Fori(1, TP // BATCH // 2) as i:
                    for s in range(2):
                        masked(2 * i + s, s)
                        reduced(2 * i + s - 1, (s - 1) % 2)
                        merged(2 * i + s - 2, s)
                reduced(TP // BATCH - 1, 1)
                merged(TP // BATCH - 2, 0)
                merged(TP // BATCH - 1, 1)
            dve.wait_ge(sem("mx_done"), km * (TP // 4) + 4)
            dve.sem_inc(sem("dve_turn"), 1)
            vec.tensor_tensor(maxima[2], maxima[2], maxima[3], ALU.max)
            link(vec.tensor_tensor(maxB, maxB, maxima[1], ALU.max))
            link(vec.tensor_tensor(maxB, maxB, maxima[2], ALU.max))
            lookup("max_edge", maxB, MAXE)
            vec.tensor_tensor(WGT[:, :], ALPHA, MAXE, ALU.subtract).then_inc(sem("exp_in"), 1)
            dve.wait_ge(sem("wgt_made"), 1)
            dve.sem_inc(sem("psum_free"), 5)

            def sums(p):
                c = PASS[p]
                acc, C = c["acc"], chunks(p)
                if c["zero"]:
                    link(vec.memset(acc[:, 0:C, :], 0.0))
                if c.get("count"):
                    link(vec.memset(cnt8, 0.0))
                if c.get("lookup"):
                    link(vec.memset(WGT[:, :], 0.0))
                rounds_reset(f"p{p}")
                with dve.Fori(0, km) as k:
                    kk = dve.snap(km * p + k)
                    round_start(f"p{p}", k)

                    def select(t, s):
                        col = REL[:, bass.ds(t, 1)]
                        if c["wt"] is None:
                            ins = vec.tensor_scalar(SEL[:, s, :], iotaK[:, :], col, None, ALU.is_equal)
                        else:
                            ins = vec.tensor_scalar(SEL[:, s, :], iotaK[:, :], col, c["wt"][:, bass.ds(t, 1)], ALU.is_equal, ALU.mult)
                        if c.get("count") or c.get("lookup"):
                            ins = vec.tensor_scalar(TOH[:, s, :], iotaR[:, :], TYP[:, bass.ds(t, 1)], None, ALU.is_equal)
                        ins.then_inc(sem("s_ready"), 1)

                    def tile(t, s, q, bases):
                        select(t + AHEAD, (s + AHEAD) % 5)
                        first = bases[s]
                        dve.wait_ge(sem("mm_done"), kk * T + t + 2)
                        dve.wait_ge(sem("psum_free"), kk * T + t + 5)
                        if c.get("count"):
                            v = cnt8[:, bass.ds(first, WIN)]
                            vec.tensor_tensor(v, v, PS[0:RELS, s, 64:64 + WIN], ALU.add)
                        if c.get("lookup"):
                            vec.tensor_tensor(SCR[:, s * WIN:(s + 1) * WIN], SEL[:, s, :], PS[:, s, 64:64 + WIN], ALU.mult)
                        v = acc[:, 0:C, bass.ds(first, WIN)]
                        vec.tensor_tensor(v, v, PS[:, s, 0:C * WIN].rearrange("p (c w) -> p c w", w=WIN), ALU.add).then_inc(sem("psum_free"), 1)
                        if c.get("lookup") and s == 4:
                            dve.wait_ge(sem("psum_free"), kk * T + t + 6)
                            vec.tensor_reduce(small[:, 8:13], SCR[:, 0:5 * WIN].rearrange("p (j w) -> p j w", w=WIN), AX, ALU.add).then_inc(sem("cnt_edge"), 1)
                            n = k * (T // 5) + q
                            dve.wait_ge(sem("cnt_edge"), n * 2 + 1)
                            vec.tensor_tensor(cols(WGT, q, 5), cols(WGT, q, 5), small[:, 8:13], ALU.add).then_inc(sem("cnt_edge"), 1)
                    for t in range(AHEAD):
                        select(t, t)
                    with dve.Fori(0, T // 10) as r:
                        for h in range(2):
                            bases = windows(dve, regs[0:HALF], five(2 * r + h))
                            for j in range(HALF):
                                tile(10 * r + h * HALF + j, j, 2 * r + h, bases)
                    bases = windows(dve, regs[0:HALF], five(T // HALF - 1))
                    for j in range(HALF):
                        tile(T - HALF + j, j, T // HALF - 1, bases)
                    dve.wait_ge(sem("psum_free"), (kk + 1) * T + 5)
                    dve.sem_inc(sem("dve_turn"), 1)
                dve.sem_inc(sem("pass_end"), 1)

            def sums_by_source():
                rounds_reset("p1")
                dve.wait_ge(sem("e1_tab"), GROUPS)
                vec.tensor_copy(src_col[:, 0:T], SRC[:, 0:T]).then_inc(sem("src_col"), 1)
                with dve.Fori(0, km) as k:
                    kk = dve.snap(km + k)
                    round_start("p1", k)
                    dve.wait_ge(sem("src_col"), 1)

                    def tile(t, s, h, j):
                        if not isinstance(t, int) or t >= 5:
                            dve.wait_ge(sem("b_mm"), k * T + t - 4)
                        vec.tensor_scalar(SEL[:, s, :], iotaK[:, :], REL[:, bass.ds(t, 1)], None, ALU.is_equal)
                        row, col = src_bc[:, h, j * P:(j + 1) * P], src_col[:, bass.ds(t, 1)]
                        vec.tensor_scalar(same[:, s, :], row, col, EWT[:, bass.ds(t, 1)], ALU.is_equal, ALU.mult).then_inc(sem("s_ready"), 1)
                        vec.scalar_tensor_tensor(twins[:, j, :], row, col, before[:, :], ALU.is_equal, ALU.mult).then_inc(sem("twins"), 1)

                    def half(q, h, uses, landed):
                        n = (k * (T // HALF) + q) * (HALF + 4)
                        c = sem("twins")
                        dve.wait_ge(sem(f"src_bc{h}"), uses * 16)
                        for j in range(HALF):
                            tile(q * HALF + j, j, h, j)
                        dve.wait_ge(c, n + HALF)
                        dup, idx = small[:, 8:13], small[:, 3:8]
                        vec.tensor_reduce(dup, twins, AX, ALU.add).then_inc(c, 1)
                        vec.tensor_scalar(idx, cols(src_col, q, HALF), -1.0, spare[:, :], ALU.mult, ALU.add).then_inc(c, 1)
                        dve.wait_ge(c, n + HALF + 2)
                        vec.scalar_tensor_tensor(idx, dup, 0.5, idx, ALU.is_gt, ALU.mult).then_inc(c, 1)
                        dve.wait_ge(c, n + HALF + 3)
                        if landed is not None:
                            dve.wait_ge(sem(f"scat{h}"), landed)
                        vec.tensor_tensor(idx, idx, cols(src_col, q, HALF), ALU.add).then_inc(c, 1)
                        dve.wait_ge(c, n + HALF + 4)
                        vec.tensor_copy(cur[:, h * HALF:(h + 1) * HALF], idx).then_inc(sem("idx_ready"), 1)
                        dve.wait_ge(sem("idx_ready"), kk * (T // HALF) + q + 1)
                        dve.sem_inc(sem("dve_turn"), 1)
                    half(0, 0, k * (T // 10 + 1) + 1, None)
                    half(1, 1, k * (T // 10) + 1, None)
                    with dve.Fori(1, T // 10) as r:
                        for h in range(2):
                            half(2 * r + h, h, k * (T // 10 + (h == 0)) + r + 1, (k * (T // 10 + (h == 0)) + r) * 80)
                    half(T // HALF - 1, 0, (k + 1) * (T // 10 + 1), (k * (T // 10 + 1) + T // 10) * 80)
                    dve.sem_inc(sem("s_ready"), AHEAD)
                    dve.wait_ge(sem("b_mm"), k * T + T)
                    dve.wait_ge(sem("scat0"), (k + 1) * (80 * 63))
                    dve.wait_ge(sem("scat1"), (k + 1) * (80 * 62))
                    dve.sem_inc(sem("dve_turn"), 1)
                dve.sem_inc(sem("pass_end"), 1)

            def add_x(name, i, u, bank):
                g = 2 * i + u
                dve.wait_ge(sem("x_mm"), X_PRODUCTS[name] * GROUPS + g + 1)
                vec.tensor_tensor(cols(X, g), cols(X, g), PS[:, bank(u), :], ALU.add).then_inc(sem("x_added"), 1)

            def x_done(name):
                dve.wait_ge(sem("x_added"), X_TERMS[name] * GROUPS + GROUPS)

            def mean(name, i, u, C):
                g = 2 * i + u
                r = outst[:, u, 512:1024]
                dve.wait_ge(sem("deg"), MEANS[name] * GROUPS + g + 1)
                vec.tensor_scalar(r, PS[:, 4, :], 1.0, None, ALU.max).then_inc(sem("deg_max"), 1)
                dve.wait_ge(sem("deg_max"), MEANS[name] * GROUPS + g + 1)
                vec.reciprocal(r, r).then_inc(sem("deg_rec"), 1)
                dve.wait_ge(sem("deg_rec"), MEANS[name] * GROUPS + g + 1)
                if later(i):
                    if name == "e5":
                        dve.wait_ge(sem("x_mm"), X_PRODUCTS[name] * GROUPS + g - 1)
                    else:
                        dve.wait_ge(sem(name + "_mean_mm"), g - 1)
                for ch in range(C):
                    ins = vec.tensor_tensor(stage[:, u, ch, :], cols(ACC_A[:, ch, :], g), r, ALU.mult)
                ins.then_inc(sem(name + "_stage"), 1)

            def hidden_pre(name, i, u):
                g = 2 * i + u
                dve.wait_ge(sem(name + "_mean_mm"), g + 1)
                if later(i):
                    if name == "e4":
                        dve.wait_ge(sem("x_mm"), X_PRODUCTS[name] * GROUPS + g - 1)
                    else:
                        dve.wait_ge(sem(name + "_hid_mm"), g - 1)
                for o in range(2):
                    ins = vec.tensor_tensor(stage2[:, u, o, :], PS[:, 2 * u + o, :], cols(ACC_B[:, o, :], g), ALU.add)
                ins.then_inc(sem(name + "_pre"), 1)

            sums(0)

            def e1(i, u):
                g = 2 * i + u
                den = outst[:, u, 512:1024]
                vec.tensor_scalar(den, cols(ACC_A[:, 1, :], g), 1e-16, None, ALU.add).then_inc(sem("e1_den"), 1)
                dve.wait_ge(sem("e1_den"), g + 1)
                vec.reciprocal(den, den).then_inc(sem("den_rec"), 1)
                dve.wait_ge(sem("den_rec"), g + 1)
                if later(i):
                    dve.wait_ge(sem("x_mm"), X_PRODUCTS["e1"] * GROUPS + g - 1)
                vec.tensor_tensor(stage[:, u, 0, :], cols(ACC_A[:, 0, :], g), den, ALU.mult).then_inc(sem("e1_stage"), 1)
                add_x("e1", i, u, lambda u: 5 + u)
            group_loop(dve, e1)
            x_done("e1")
            norm_stats(1)
            group_loop(dve, lambda i, u: transposed_group(1, i, u, "e1_tab", 1))
            sums_by_source()
            def add_parts(i, u):
                dve.wait_ge(sem(f"parts_in{u}"), (i + 1) * (16 * HALF))
                for n in range(HALF):
                    if n or u or later(i):
                        dve.wait_ge(sem("parts_added"), (2 * i + u) * HALF + n)
                    ins = vec.tensor_tensor(cols(X, i), cols(X, i), parts_in[:, u, n, :], ALU.add)
                    ins.then_inc(sem("parts_added"), 1)
                if u:
                    dve.wait_ge(sem("parts_added"), (2 * i + u + 1) * HALF)
                    dve.sem_inc(sem("x_added"), 1)
            for u in range(2):
                add_parts(0, u)
            with dve.Fori(1, GROUPS) as i:
                for u in range(2):
                    add_parts(i, u)
            x_done("e2")
            norm_stats(2)
            group_loop(dve, lambda i, u: transposed_group(2, i, u, "ln2_root", 1))
            sums(2)
            def e3(i, u):
                g = 2 * i + u
                mean("e3", i, u, 1)
                hidden_pre("e3", i, u)
                dve.wait_ge(sem("e3_hid_mm"), g + 1)
                for o in range(2):
                    v = cols(ACC_B[:, o, :], g)
                    ins = vec.scalar_tensor_tensor(v, PS[:, 2 * u + o, :], bcol[:, 1, o:o + 1], stage2[:, u, o, :], ALU.add, ALU.add)
                ins.then_inc(sem("e3_root"), 1)
            group_loop(dve, e3)
            dve.wait_ge(sem("e3_root"), GROUPS)
            sums(3)
            dve.wait_ge(sem("cnt_edge"), km * (2 * (T // 5)))
            link(vec.tensor_scalar(WGT[:, :], WGT[:, :], 1.0, None, ALU.max))
            link(vec.reciprocal(WGT[:, :], WGT[:, :]))

            def e4(i, u):
                mean("e4", i, u, 2)
                hidden_pre("e4", i, u)
                add_x("e4", i, u, lambda u: 6)
            group_loop(dve, e4)
            x_done("e4")
            sums(4)
            def e5(i, u):
                mean("e5", i, u, 1)
                add_x("e5", i, u, lambda u: 5 + u)
            group_loop(dve, e5)
            x_done("e5")
            norm_stats(3)

            def unit_out(p, i, u, j):
                g = 2 * i + u
                per = 4 * FIRST_TABLES[p][1]
                dve.wait_ge(sem("unit"), UNITS[p] + g * per + j + 1)
                if later(i) or u or j >= 2:
                    dve.wait_ge(sem(f"unit_stored{j % 2}"), 16 * (UNITS[p] // 2 + g * (per // 2) + j // 2))
                vec.tensor_copy(outst[:, j % 2, 512:1024], PS[:, 2 * (j % 2) + 1, :]).then_inc(sem("unit_outd"), 1)

            def t5(i, u):
                transposed_group(3, i, u, "unit", 8)
                for j in range(8):
                    unit_out(5, i, u, j)
            group_loop(dve, t5)
            sums(5)
            def t6(i, u):
                for j in range(8):
                    unit_out(6, i, u, j)
            group_loop(dve, t6)
            sums(6)
            def t7(i, u):
                for j in range(4):
                    unit_out(7, i, u, j)
                add_x("t7", i, u, lambda u: 4)
            group_loop(dve, t7)
            x_done("t7")
            sums(7)
            group_loop(dve, lambda i, u: add_x("e8", i, u, lambda u: 5 + u))
            x_done("e8")
            dve.sem_inc(sem("x_final"), 1)

        @block.tensor
        def _(pe):
            mm = nc.tensor.matmul

            pe.wait_ge(sem("const"), 8)
            pe.wait_ge(sem("rows_loaded"), 64)
            pe.wait_ge(sem("rows_made"), 4)
            for n, v in enumerate((src_f, typ_f, rel_f, ewt_r)):
                for b in range(RB):
                    ins = nc.tensor.transpose(PS[:, 2 * n + b // 4, (b % 4) * RQ:(b % 4 + 1) * RQ], v[:, b, :], ident[0:RQ, 0:RQ])
                ins.then_inc(sem("rows_tr"), 1)
            pe.wait_ge(sem("cols_done"), 10)
            pe.wait_ge(sem("w_loaded"), 16 * 28)
            for n in range(18):
                ins = nc.tensor.transpose(PS[:, n // 4, (n % 4) * P:(n % 4 + 1) * P], wraw[:, n, :], ident[:, :])
            ins.then_inc(sem("wT_tr"), 1)
            nc.tensor.transpose(PS[0:1, 5, 0:RQ], span_f, ident[0:RQ, 0:RQ]).then_inc(sem("span_tr"), 1)
            pe.wait_ge(sem("vB_made"), 1)
            mm(PS[:, 6, 0:EDIM], vB[:, :], ident[0:EDIM, 0:EDIM], start=True, stop=True).then_inc(sem("vrow_mm"), 1)

            def transpose_group(k, i, u):
                g = 2 * i + u
                pe.wait_ge(sem("ln_h"), k * GROUPS + g + 1)
                if later(i):
                    pe.wait_ge(sem("ln_ht"), k * GROUPS + g - 1)
                for q in range(4):
                    ins = nc.tensor.transpose(PS[:, 5 + u, q * P:(q + 1) * P], stage[:, u, 0, q * P:(q + 1) * P], ident[:, :])
                ins.then_inc(sem("ln_tr"), 1)
                pe.wait_ge(sem("ln_ht"), k * GROUPS + g + 1)

            pe.wait_ge(sem("wdst_made"), 1)
            pe.wait_ge(sem("spans_known"), 1)
            pe.wait_ge(sem("ea_used"), 1)
            pe.wait_ge(sem("wT_done"), 7)

            def l0(i, u):
                g = 2 * i + u
                transpose_group(0, i, u)
                if later(i):
                    pe.wait_ge(sem("asrow_done"), g - 1)
                    pe.wait_ge(sem("adst_done"), g - 1)
                mm(PS[0:1, u, :], watt[:, 0:1], stage2[:, u, 0, :], start=True, stop=True)
                mm(PS[:, 2 + u, :], wdst[:, :], stage2[:, u, 0, :], start=True, stop=True).then_inc(sem("ln0_mm"), 1)
            group_loop(pe, l0)
            pe.wait_ge(sem("aed_loaded"), 16)
            pe.wait_ge(sem("ln_ht"), GROUPS)
            for b in range(RB):
                ins = nc.tensor.transpose(PS[:, 5 + b // 4, (b % 4) * RQ:(b % 4 + 1) * RQ], aed_r[:, b, :], ident[0:RQ, 0:RQ])
            ins.then_inc(sem("aed_tr"), 1)

            pe.wait_ge(sem("logits_loaded"), 16)
            pe.wait_ge(sem("asrow_done"), GROUPS)
            pe.wait_ge(sem("adst_done"), GROUPS)

            def rows_of_logits(i, s):
                q = 5 * i + s
                pe.wait_ge(sem("hot_made"), q + 1)
                if later(i):
                    pe.wait_ge(sem("picked"), q - 4)
                for j in range(5):
                    ins = mm(PS[:, s, j * LO:(j + 1) * LO], hot_hi[:, s, j * P:(j + 1) * P], logit_tab, start=True, stop=True)
                ins.then_inc(sem("src_mm"), 1)
            for s in range(5):
                rows_of_logits(0, s)
            with pe.Fori(1, 25) as i:
                for s in range(5):
                    rows_of_logits(i, s)

            km = rounds(pe)
            pe.wait_ge(sem("picked"), T // 5)
            with pe.Fori(0, km) as k:
                def turned(g, s):
                    pe.wait_ge(sem("mx_masked"), k * (TP // BATCH) + g + 1)
                    for q in range(4):
                        ins = nc.tensor.transpose(PS[:, s, q * P:(q + 1) * P], pen[:, s, q * P:(q + 1) * P], ident[:, :])
                    ins.then_inc(sem("mx_tr"), 1)

                def spread(g, s):
                    pe.wait_ge(sem("mx_diag"), k * (TP // BATCH) + g + 1)
                    mm(PS[:, 2 + s, :], ones[:, :], diag[:, s, :], start=True, stop=True).then_inc(sem("mx_all"), 1)
                turned(0, 0)
                turned(1, 1)
                spread(0, 0)
                with pe.Fori(1, TP // BATCH // 2) as i:
                    for s in range(2):
                        turned(2 * i + s, s)
                        spread(2 * i + s - 1, (s - 1) % 2)
                spread(TP // BATCH - 1, 1)

            regs = window_regs(pe, "pe")

            def sums(p):
                c = PASS[p]
                C = c["F"] // P
                with pe.Fori(0, km) as k:
                    kk = pe.snap(km * p + k)
                    kr = pe.snap(km * (p - (p > 1)) + k)
                    if c.get("lookup"):
                        pe.wait_ge(sem("round"), (km * 3 + 1) * ROUNDS.index(f"p{p}") + k * 3 + 4)

                    def onehot_tr(t, s):
                        pe.wait_ge(sem("s_ready"), kk * (T + AHEAD) + t + 1)
                        nc.tensor.transpose(PS[0:RELS, s, P:2 * P], TOH[:, s, :], ident[:, :]).then_inc(sem("toh_tr"), 1)

                    def tile(t, s, slot, use, bases, left=T):
                        if c.get("lookup") and left > 2:
                            onehot_tr(t + 2, (s + 2) % 5)
                        pe.wait_ge(sem(f"row{slot}"), use * 16)
                        pe.wait_ge(sem("s_ready"), kk * (T + AHEAD) + t + 1)
                        pe.wait_ge(sem("psum_free"), kk * T + t + 1)
                        if c.get("count"):
                            mm(PS[0:RELS, s, 64:64 + WIN], TOH[:, s, :], SEL[:, s, :], start=True, stop=True)
                        if c.get("lookup"):
                            pe.wait_ge(sem("toht_made"), k * T + t + 1)
                            mm(PS[:, s, 64:64 + WIN], TOHT[:, s, :], cnt8[:, bass.ds(bases[s], WIN)], start=True, stop=True)
                        for ch in range(C):
                            ins = mm(PS[:, s, ch * WIN:(ch + 1) * WIN], ring[:, slot, ch * P:(ch + 1) * P], SEL[:, s, :], start=True, stop=True)
                        if c["ones"]:
                            ins = mm(PS[:, s, WIN:2 * WIN], ones[:, :], SEL[:, s, :], start=True, stop=True)
                        ins.then_inc(sem("mm_done"), 1)
                    if c.get("lookup"):
                        onehot_tr(0, 0)
                        onehot_tr(1, 1)
                    with pe.Fori(0, T // 10) as r:
                        for h in range(2):
                            bases = windows(pe, regs, five(2 * r + h)) if c.get("lookup") else None
                            for j in range(HALF):
                                tile(10 * r + h * HALF + j, j, h * HALF + j, kr * (T // 10 + (h == 0)) + r + 1, bases)
                    bases = windows(pe, regs, five(T // HALF - 1)) if c.get("lookup") else None
                    for j in range(HALF):
                        tile(T - HALF + j, j, j, (kr + 1) * (T // 10 + 1), bases, HALF - j)

            def out_x(name, terms_of, bias, bank, ready):
                def body(i, u):
                    g = 2 * i + u
                    pe.wait_ge(sem(name + ready), g + 1)
                    if later(i):
                        pe.wait_ge(sem("x_added"), X_TERMS[name] * GROUPS + g - 1)
                    x_term(name, i, u, terms_of, bias, bank)
                return body

            def x_term(name, i, u, terms_of, bias, bank):
                for q in range(4):
                    dst = PS[:, bank(u), q * P:(q + 1) * P]
                    terms = terms_of(u, q)
                    for n, (lhs, rhs) in enumerate(terms):
                        ins = mm(dst, lhs, rhs, start=n == 0, stop=bias is None and n == len(terms) - 1)
                    if bias is not None:
                        ins = mm(dst, ones[0:1, :], brow[0:1, bias, :], start=False, stop=True)
                ins.then_inc(sem("x_mm"), 1)

            def staged(v, u, ch, q):
                return v[:, u, ch, q * P:(q + 1) * P]

            def degrees(name, i, u):
                g = 2 * i + u
                if later(i) or u:
                    pe.wait_ge(sem("deg_max"), MEANS[name] * GROUPS + g)
                mm(PS[:, 4, :], ones[0:RELS, :], cols(cnt8, g), start=True, stop=True).then_inc(sem("deg"), 1)
                pe.wait_ge(sem(name + "_stage"), g + 1)

            def root(name, w, i, u, bank_of, src, kc, ready, emptied, lag, before=0):
                g = 2 * i + u
                pe.wait_ge(sem(ready), before + g + 1)
                if later(i) or (u and lag == 1):
                    pe.wait_ge(sem(emptied), g + 1 - lag)
                for o in range(2):
                    for ch in range(kc):
                        lhs = w[:, o * P:(o + 1) * P] if kc == 1 else w[:, ch, o * P:(o + 1) * P]
                        ins = mm(PS[:, bank_of(o), :], lhs, src[:, u, ch, :], start=ch == 0, stop=ch == kc - 1)
                ins.then_inc(sem(name), 1)

            sums(0)
            pe.wait_ge(sem("pass_end"), 1)
            group_loop(pe, out_x("e1", lambda u, q: [(staged(stage, u, 0, q), W0[:, :])], 0, lambda u: 5 + u, "_stage"))
            def l1(i, u):
                g = 2 * i + u
                transpose_group(1, i, u)
                if later(i):
                    pe.wait_ge(sem("e1_out"), g - 1)
                for q in range(4):
                    ins = mm(PS[:, 2 + u, q * P:(q + 1) * P], staged(stage2, u, 0, q), W1[:, :], start=True, stop=True)
                ins.then_inc(sem("e1_tab"), 1)
            group_loop(pe, l1)
            with pe.Fori(0, km) as k:
                kk = pe.snap(km + k)

                def window_by_source(t, s):
                    pe.wait_ge(sem("s_ready"), kk * (T + AHEAD) + t + 1)
                    mm(PS[0:WIN, s, 0:P], SEL[:, s, :], same[:, s, :], start=True, stop=True).then_inc(sem("b_mm"), 1)

                def tile(t, s, slot, use, last=False):
                    if not last:
                        window_by_source(t + 1, (s + 1) % 5)
                    pe.wait_ge(sem("b_ready"), k * T + t + 1)
                    pe.wait_ge(sem(f"window{slot // 5}"), use * 80)
                    pe.wait_ge(sem("psum_free"), kk * T + t + 1)
                    mm(PS[:, s, P:2 * P], spread_t[:, s, :], ring[0:WIN, slot, D:2 * D], start=True, stop=True).then_inc(sem("mm_done"), 1)
                window_by_source(0, 0)
                with pe.Fori(0, T // 10) as r:
                    for j in range(10):
                        tile(10 * r + j, j % 5, j, k * (T // 10 + (j < 5)) + r + 1)
                for j in range(5):
                    tile(T - 5 + j, j, j, (k + 1) * (T // 10 + 1), j == 4)
            def l2(i, u):
                transpose_group(2, i, u)
                root("ln2_root", Wr1T, i, u, lambda o: 2 * u + o, stage2, 1, "ln_ht", "ln2_rooted", 2, 2 * GROUPS)
            group_loop(pe, l2)
            sums(2)
            pe.wait_ge(sem("pass_end"), 3)
            def e3(i, u):
                g = 2 * i + u
                degrees("e3", i, u)
                root("e3_mean_mm", Wl1T, i, u, lambda o: 2 * u + o, stage, 1, "e3_stage", "e3_root", 2)
                pe.wait_ge(sem("e3_hid"), g + 1)
                for j in range(2):
                    if later(i) or u:
                        pe.wait_ge(sem("e3_out"), 2 * g + j - 1)
                    for q in range(2):
                        for o in range(2):
                            ins = nc.tensor.transpose(PS[:, 5 + j, q * HID + o * P:q * HID + (o + 1) * P],
                                                      staged(stage2, u, o, 2 * j + q), ident[:, :])
                    ins.then_inc(sem("e3_tr"), 1)
                root("e3_hid_mm", Wr2T, i, u, lambda o: 2 * u + o, stage2, 2, "e3_hid", "e3_root", 2)
            group_loop(pe, e3)
            sums(3)
            pe.wait_ge(sem("pass_end"), 4)
            def e4(i, u):
                g = 2 * i + u
                degrees("e4", i, u)
                root("e4_mean_mm", Wl2T, i, u, lambda o: 2 * u + o, stage, 2, "e4_stage", "e4_pre", 2)
                pe.wait_ge(sem("e4_hid"), g + 1)
                if later(i) or u:
                    pe.wait_ge(sem("e4_out"), g)
                for q in range(4):
                    for ch in range(2):
                        ins = mm(PS[:, 5, q * P:(q + 1) * P], staged(stage2, u, ch, q), Wl3T[:, ch, :], start=ch == 0, stop=ch == 1)
                ins.then_inc(sem("e4_tab"), 1)
                if later(i) or u:
                    pe.wait_ge(sem("x_added"), X_TERMS["e4"] * GROUPS + g)
                x_term("e4", i, u, lambda u, q: [(staged(stage2, u, ch, q), w[:, ch, :]) for w in (Wr3T, WpjT) for ch in range(2)],
                       1, lambda u: 6)
            group_loop(pe, e4)
            sums(4)
            pe.wait_ge(sem("pass_end"), 5)
            def e5(i, u):
                g = 2 * i + u
                degrees("e5", i, u)
                if later(i):
                    pe.wait_ge(sem("x_added"), X_TERMS["e5"] * GROUPS + g - 1)
                for q in range(4):
                    ins = nc.tensor.transpose(PS[:, 5 + u, q * P:(q + 1) * P], staged(stage, u, 0, q), ident[:, :])
                ins.then_inc(sem("x_mm"), 1)
            group_loop(pe, e5)

            def units(p, i, u, src):
                kc, halves, width = FIRST_TABLES[p]
                g = 2 * i + u
                per = 4 * halves
                for j in range(per):
                    b, h = j // halves, j % halves
                    if later(i) or u or j >= 2:
                        pe.wait_ge(sem("unit_outa"), UNITS[p] + g * per + j - 1)
                        pe.wait_ge(sem("unit_outd"), UNITS[p] + g * per + j - 1)
                    for n in range(2):
                        at = h * 1024 + n * 512
                        for ch in range(kc):
                            ins = mm(PS[:, 2 * (j % 2) + n, :], staged(src, u, ch, b), relw[:, ch * width + at:ch * width + at + 512],
                                     start=ch == 0, stop=ch == kc - 1)
                    ins.then_inc(sem("unit"), 1)

            pe.wait_ge(sem("relw_loaded"), 16)

            def t5(i, u):
                transpose_group(3, i, u)
                root("t5_root", root1, i, u, lambda o: 4 + 3 * o, stage2, 1, "ln_ht", "t5_rooted", 1, 3 * GROUPS)
                units(5, i, u, stage2)
            group_loop(pe, t5)
            sums(5)
            pe.wait_ge(sem("relw_loaded"), 48)

            def t6(i, u):
                root("t6_root", root2, i, u, lambda o: 4 + 3 * o, stage2, 2, "t6_hid", "t6_rooted", 1)
                units(6, i, u, stage2)
            group_loop(pe, t6)
            sums(6)
            pe.wait_ge(sem("relw_loaded"), 80)

            def t7(i, u):
                g = 2 * i + u
                pe.wait_ge(sem("t7_hid"), g + 1)
                units(7, i, u, stage2)
                if later(i) or u:
                    pe.wait_ge(sem("x_added"), X_TERMS["t7"] * GROUPS + g)
                x_term("t7", i, u, lambda u, q: [(staged(stage2, u, ch, q), root3[:, ch, :]) for ch in range(2)], 2, lambda u: 4)
            group_loop(pe, t7)
            sums(7)
            def e8(i, u):
                g = 2 * i + u
                pe.wait_ge(sem("e8_stage"), g + 1)
                if later(i):
                    pe.wait_ge(sem("x_added"), X_TERMS["e8"] * GROUPS + g - 1)
                for q in range(4):
                    ins = nc.tensor.transpose(PS[:, 5 + u, q * P:(q + 1) * P], staged(stage, u, 0, q), ident[:, :])
                ins.then_inc(sem("x_mm"), 1)
            group_loop(pe, e8)


def kernel(**inputs):
    import numpy as np
    import concourse.bacc as bacc
    from concourse.bass_utils import run_bass_kernel_spmd as run

    nc = bacc.Bacc("TRN2", target_bir_lowering=False, num_devices=1)
    arrays, args = {}, {}
    for name in sorted(inputs):
        v = np.ascontiguousarray(inputs[name])
        arrays["in_" + name] = v
        args[name] = nc.dram_tensor("in_" + name, v.shape, mybir.dt.from_np(v.dtype), kind="ExternalInput").ap()
    out = nc.dram_tensor("out_0", (N, D), F32, kind="ExternalOutput").ap()
    build(nc, args, out)
    return run(nc, [arrays], core_ids=[0]).results[0]["out_0"]
```

```python
from contextlib import ExitStack

import concourse.bass as bass
from concourse import mybir
from concourse.alu_op_type import AluOpType as ALU

F32, I32, BF16 = mybir.dt.float32, mybir.dt.int32, mybir.dt.bfloat16
ACT = mybir.ActivationFunctionType
AX = mybir.AxisListType.X

P = 128
N, D, HID = 5000, 128, 256
EDGES, EDIM, RELS = 80000, 32, 8
T = EDGES // P
RQ, RB = 125, 5
BLOCKS = -(-N // P)
NP = BLOCKS * P
GN = 4 * P
GROUPS = NP // GN
WIN = 32
WIN_SHIFT = 5
TP = 640
LO = 64
HI = NP // LO
AHEAD = 3
BATCH = 16
HALF = 5
NEG = -1.0e30


def build(nc, a, out):
    ctx = ExitStack()
    with ctx:
        def sb(name, shape, dt=F32):
            return ctx.enter_context(nc.sbuf_tensor(name, shape, dt))

        made = {}

        def sem(name):
            if name not in made:
                made[name] = ctx.enter_context(nc.semaphore(name))
            return made[name]


        X = sb("X", [P, NP])
        ACC_A = sb("ACC_A", [P, 2, NP])
        ACC_B = sb("ACC_B", [P, 2, NP])
        MULTI = sb("MULTI", [P, NP])
        SCR = sb("SCR", [P, 6144])
        REL = sb("REL", [P, TP])
        SRC = sb("SRC", [P, TP], I32)
        KEY = sb("KEY", [P, TP], I32)
        TYP = sb("TYP", [P, TP])
        EWT = sb("EWT", [P, TP])
        WGT = sb("WGT", [P, TP])
        BASEF = sb("BASEF", [1, TP])
        BASEK = sb("BASEK", [1, TP // 5 * 8], I32)
        BASE16 = sb("BASE16", [1, TP], I32)
        cur = sb("cur", [P, 2 * HALF], I32)
        ring = sb("ring", [P, 2 * HALF, HID])
        SEL = sb("SEL", [P, 5, WIN])
        TOH = sb("TOH", [P, 5, RELS])
        zeros = sb("zeros", [P, D])
        ident = sb("ident", [P, P])
        ones = sb("ones", [P, P])
        iotaW = sb("iotaW", [P, WIN])
        iotaK = sb("iotaK", [P, WIN])
        iotaL = sb("iotaL", [P, LO])
        iotaR = sb("iotaR", [P, RELS])
        part = sb("part", [P, 1])
        minus_part = sb("minus_part", [P, 1])
        spare = sb("spare", [P, 1])
        koff = sb("koff", [P, 1])
        spans = sb("spans", [1, 1], I32)
        stats = sb("stats", [P, 4, 6])
        group_mv = sb("group_mv", [P, 4, 2])
        mv = sb("mv", [P, BLOCKS, 2])
        std = sb("std", [P, BLOCKS])
        rstd = sb("rstd", [P, BLOCKS])
        shift = sb("shift", [P, BLOCKS])
        small = sb("small", [P, 3 * BATCH])
        W0 = sb("W0", [P, D])
        W1 = sb("W1", [P, D])
        Wl1T = sb("Wl1T", [P, HID])
        Wr1T = sb("Wr1T", [P, HID])
        Wl2T = sb("Wl2T", [P, 2, HID])
        Wr2T = sb("Wr2T", [P, 2, HID])
        W3T = sb("W3T", [P, 2, 2 * D])
        root1 = sb("root1", [P, HID])
        root2 = sb("root2", [P, 2, HID])
        root3 = sb("root3", [P, 2, D])
        brow = sb("brow", [1, 2, D])
        bcol = sb("bcol", [P, 5, 2])
        att = sb("att", [P, 4, D])
        before = sb("before", [P, P])
        watt = sb("watt", [P, 2])
        wdst = sb("wdst", [P, P])
        we_sb = sb("we_sb", [EDIM, D])
        vB = sb("vB", [EDIM, P])
        vrow = sb("vrow", [P, EDIM])
        PS = ctx.enter_context(nc.psum_tensor("PS", [P, 8, 512], F32))

        stage = SCR[:, 0:2048].rearrange("p (u c n) -> p u c n", u=2, c=2)
        stage2 = SCR[:, 2048:4096].rearrange("p (u c n) -> p u c n", u=2, c=2)
        outst = SCR[:, 4096:6144].rearrange("p (u n) -> p u n", u=2)
        two = SCR.rearrange("p (v k n) -> p v k n", v=6, n=512)

        def unit_slot(p, j):
            if j % 4 < 2:
                return two[:, 4 + j % 4]
            if p == 5:
                return (stage, stage2)[j % 2][:, :, 1, :]
            return two[:, j % 4 - 2]
        wraw = SCR[:, 0:18 * P].rearrange("p (k f) -> p k f", f=P)
        hot_hi = SCR[:, 0:1600].bitcast(BF16)[0:HI, :].rearrange("p (s e) -> p s e", s=5)
        hi_bc = SCR[:, 3200:4800].bitcast(BF16)[0:HI, :].rearrange("p (s e) -> p s e", s=5)

        e4_out = PS[:, 5:7, :].rearrange("p b (q n) -> p (b q) n", n=2 * D)
        rdeg = ACC_B[:, 0, :]

        flatA = ACC_A[:, :, :].rearrange("p c n -> p (c n)")
        flatB = ACC_B[:, :, :].rearrange("p c n -> p (c n)")

        def row_array(k, dt=F32):
            v = flatA[0:RQ, k * 640:(k + 1) * 640]
            return (v if dt == F32 else v.bitcast(dt)).rearrange("q (b j) -> q b j", b=RB)

        src_r, dst_r, typ_r = (row_array(k, I32) for k in range(3))
        ewt_r, src_f, dst_f, rel_f, typ_f = (row_array(k) for k in range(3, 8))
        hi_i = row_array(8, I32)
        aed_r = row_array(9)
        hi_b = flatA[0:RQ, 6400:6720].bitcast(BF16).rearrange("q (b j) -> q b j", b=RB)
        base_f = flatA[0:RQ, 6720:6725]
        high_f = flatA[0:RQ, 6725:6730]
        span_f = flatA[0:RQ, 6730:6731]
        aflat = flatA[:, 6800:7425]
        ea = [flatB[:, 4000 * u:4000 * (u + 1)] for u in range(2)]
        logit_part = SCR[:, 4800:4800 + 3 * LO // 2].bitcast(BF16)[0:HI, :].rearrange("p (k l) -> p k l", k=3)
        logit_rest = SCR[0:HI, 4900:4900 + LO]
        picks = flatA[:, 7500:7500 + 25 * LO].rearrange("p (s j l) -> p s j l", s=5, l=LO)
        logit_tab = SCR[0:HI, 5000:5000 + LO]
        asrow = flatA[0:1, 0:NP]
        diag = SCR[:, 5120:6144].rearrange("p (u n) -> p u n", u=2)
        maxB = ACC_B[:, 0, :]
        adstB = ACC_B[:, 1, :]
        maxima = [maxB, ACC_B[:, 1, :], ACC_A[:, 0, :], ACC_A[:, 1, :]]
        src_bc = SCR[:, 0:1280].bitcast(I32).rearrange("p (u e) -> p u e", u=2)
        same = SCR[:, 1280:1920].rearrange("p (s e) -> p s e", s=5)
        spread_t = SCR[0:WIN, 1920:2560].rearrange("p (s e) -> p s e", s=5)
        src_col = SCR[:, 2560:3200]
        row_col = MULTI[:, 0:T]
        row_low, row_high = (MULTI[:, k * TP:k * TP + T].bitcast(I32) for k in (1, 2))
        twins = SCR[:, 3200:3840].rearrange("p (s e) -> p s e", s=5)
        TOHT = SCR[0:RELS, 0:1280].rearrange("p (u e) -> p u e", u=2)
        typ_bc = SCR[0:RELS, 2560:3840].bitcast(I32).rearrange("p (u e) -> p u e", u=2)
        hits = SCR[:, 3840:3840 + HALF * WIN]
        parts_in = SCR[:, 0:5120].rearrange("p (u r n) -> p u r n", u=2, r=5)
        ASRC, ADST, MAXE, AEDG, SLO, ALPHA = (MULTI[:, k * TP:(k + 1) * TP] for k in range(6))
        lk = MULTI[:, 6 * TP:6 * TP + 2 * BATCH * WIN]
        place = lk.rearrange("p (u j w) -> p u j w", u=2, w=WIN)
        pen = MULTI[:, 6 * TP:6 * TP + 2 * BATCH * WIN].rearrange("p (u n) -> p u n", u=2)
        cnt8 = MULTI[0:RELS, :]
        relw = MULTI[:, 0:4096]

        def dram(name, shape, dt=F32):
            return nc.dram_tensor(name, shape, dt).ap()

        base_d = dram("base_d", (TP,))
        hi_d = dram("hi_d", (EDGES,), BF16)
        aed_d = dram("aed_d", (EDGES,))
        tab = [dram("tab_l0", (NP, D)), dram("tab_l1", (NP, D)), dram("tab_l2a", (NP, D)),
               dram("tab_l2b", (NP, HID)), dram("tab_l2c", (NP, D)), dram("tab_l3a", (NP * RELS, HID)),
               dram("tab_l3b", (NP * RELS, HID)), dram("tab_l3c", (NP * RELS, D))]

        part_d = [dram(f"part_{n}", (NP + P, D)) for n in range(2 * HALF)]

        PASS = [dict(F=D, idx=SRC, wt=WGT, acc=ACC_A, ones=True, zero=True),
                dict(F=D, idx=SRC, wt=EWT, acc=ACC_A, ones=False, zero=True),
                dict(F=D, idx=SRC, wt=None, acc=ACC_A, ones=False, zero=True, count=True),
                dict(F=HID, idx=SRC, wt=None, acc=ACC_A, ones=False, zero=True),
                dict(F=D, idx=SRC, wt=None, acc=ACC_A, ones=False, zero=True, lookup=True),
                dict(F=HID, idx=KEY, wt=WGT, acc=ACC_A, ones=False, zero=False),
                dict(F=HID, idx=KEY, wt=WGT, acc=ACC_B, ones=False, zero=False),
                dict(F=D, idx=KEY, wt=WGT, acc=ACC_A, ones=False, zero=False)]

        def chunks(p):
            return 2 if PASS[p]["F"] == HID or PASS[p]["ones"] else 1

        def rows_of(v):
            return v.rearrange("(b q j) -> q b j", q=RQ, j=P)

        def group_loop(eng, body):
            for u in range(2):
                body(0, u)
            with eng.Fori(1, GROUPS // 2) as i:
                for u in range(2):
                    body(i, u)

        def following(i, u):
            if isinstance(i, int) and 2 * i + u + 1 == GROUPS:
                return None
            return i + u, 1 - u

        def ahead_loop(eng, first, body):
            def turn(i, u):
                if following(i, u):
                    first(*following(i, u))
                body(i, u)
            first(0, 0)
            for u in range(2):
                turn(0, u)
            with eng.Fori(1, GROUPS // 2 - 1) as i:
                for u in range(2):
                    turn(i, u)
            for u in range(2):
                turn(GROUPS // 2 - 1, u)

        def later(i):
            return not isinstance(i, int) or i > 0

        def cols(v, g, n=GN):
            return v[:, bass.ds(g * n, n)]

        def cols2(v, g):
            return v[:, :, bass.ds(g * GN, GN)]

        class Chain:

            def __init__(self, eng, name, base=0):
                self.eng, self.s, self.n = eng, sem(name), base

            def __call__(self, ins):
                ins.then_inc(self.s, 1)
                self.n = self.n + 1
                self.eng.wait_ge(self.s, self.n)

        def rounds(eng):
            eng.wait_ge(sem("spans_known"), 1)
            return eng.value_load(spans[0:1, 0:1], min_val=1, max_val=NP // WIN + 1)

        def window_regs(eng, who, n=HALF):
            return [eng.alloc_register(name=f"{who}_window{j}") for j in range(n)]

        def windows(eng, regs, first):
            eng.load(regs, first)
            return [eng.snap(r, min_val=0, max_val=NP - WIN) for r in regs]

        def five(q):
            return BASEK[0:1, bass.ds(q * 8, HALF)]

        block = ctx.enter_context(nc.Block())

        FIRST_TABLES = {5: (1, 2, 2048), 6: (2, 2, 2048), 7: (2, 1, 1024)}

        STORED = {0: 0, 1: 1, 2: 2, 4: 3}
        UNITS = {5: 0, 6: 8 * GROUPS, 7: 16 * GROUPS}
        ROUNDS = ["adst", "max", "max_edge"] + [f"p{p}" for p in range(8)]
        X_TERMS = {n: k for k, n in enumerate(("e1", "e2", "e4", "e5", "e8"))}
        X_PRODUCTS = {n: k for k, n in enumerate(("e1", "e4", "e5", "e8"))}
        MEANS = {n: k for k, n in enumerate(("e3", "e4"))}

        def table_ready(p):
            half = 16 * GROUPS // 2
            if p in STORED:
                return [(sem(f"group_stored{u}"), (STORED[p] + 1) * half) for u in range(2)]
            if p == 3:
                return [(sem(f"e3_stored{u}"), 2 * half) for u in range(2)]
            return [(sem(f"unit_stored{s}"), 16 * (UNITS[p] // 4 + GROUPS * FIRST_TABLES[p][1])) for s in range(4)]

        @block.sync
        def _(sp):
            def load(dst, src, s):
                sp.dma_start(dst, src, allow_slow_non_contiguous=True).then_inc(sem(s), 16)

            for v, name in ((src_r, "src"), (dst_r, "dst"), (typ_r, "edge_type_8"), (ewt_r, "edge_weight")):
                load(v, rows_of(a[name]), "rows_loaded")
            full = N // P
            sp.wait_ge(sem("x_padded"), 1)
            load(X[:, 0:full * P].rearrange("p (b f) -> p b f", f=D),
                 a["x"][0:full * P, :].rearrange("(b p) f -> p b f", p=P), "x_loaded")
            load(X[0:N - full * P, full * P:NP], a["x"][full * P:N, :], "x_loaded")
            for k, name in enumerate(("att_src", "att_dst", "att_edge")):
                load(att[:, k, :], a["L0_gnn_" + name].rearrange("(o f) -> o f", o=1).to_broadcast([P, D]), "w_loaded")
            load(att[:, 3, :], a["L1_gnn_bias"].rearrange("(o f) -> o f", o=1).to_broadcast([P, D]), "w_loaded")
            load(W0[:, :], a["L0_gnn_W"], "w_loaded")
            load(we_sb[:, :], a["L0_gnn_W_edge"], "w_loaded")
            load(W1[:, :], a["L1_gnn_weight"], "w_loaded")
            at = 0
            for name, oc, fc in (("W_l1", 2, 1), ("W_r1", 2, 1), ("W_l2", 2, 2), ("W_r2", 2, 2),
                                 ("W_l3", 1, 2), ("W_r3", 1, 2), ("W_proj", 1, 2)):
                for o in range(oc):
                    load(wraw[:, at:at + fc, :], a["L2_gnn_" + name][o * P:(o + 1) * P, :]
                         .rearrange("o (c f) -> o c f", f=P), "w_loaded")
                    at += fc
            load(root1[:, :], a["L3_gnn_root1"], "w_loaded")
            load(root2[:, :, :], a["L3_gnn_root2"].rearrange("(c p) o -> p c o", p=P), "w_loaded")
            load(root3[:, :, :], a["L3_gnn_root3"].rearrange("(c p) o -> p c o", p=P), "w_loaded")
            for k, name in enumerate(("L0_gnn_bias", "L2_gnn_b_l3")):
                load(brow[0:1, k, :], a[name].rearrange("(o f) -> o f", o=1), "w_loaded")
            for k, name in enumerate(("L2_gnn_b_l1", "L2_gnn_b_l2", "L3_gnn_b1", "L3_gnn_b2")):
                load(bcol[:, k, :], a[name].rearrange("(c p) -> p c", p=P), "w_loaded")
            load(bcol[:, 4, 0:1], a["L3_gnn_b3"].rearrange("(p o) -> p o", o=1), "w_loaded")
            ea_v = a["edge_attr_32"].rearrange("(p c j) f -> c p (j f)", p=P, c=5)
            for c in range(5):
                if c >= 2:
                    sp.wait_ge(sem("ea_used"), c - 1)
                sp.dma_start(ea[c % 2], ea_v[c]).then_inc(sem(f"ea_loaded{c % 2}"), 16)
            sp.wait_ge(sem("base_made"), 1)
            load(base_d[0:T].rearrange("(b q) -> q b", q=RQ), base_f, "base_stored")
            sp.wait_ge(sem("base_stored"), 16)
            sp.wait_ge(sem("x_padded"), 2)
            load(BASEF[:, 0:T], base_d[0:T].rearrange("(o t) -> o t", o=1), "base_loaded")
            sp.wait_ge(sem("hi_made"), 1)
            load(rows_of(hi_d), hi_b, "hi_stored")
            sp.wait_ge(sem("aed_made"), 5)
            load(aed_d.rearrange("(p j) -> p j", p=P), aflat, "aed_stored")
            sp.wait_ge(sem("aed_stored"), 16)
            load(aed_r, rows_of(aed_d), "aed_loaded")

            def store_h(k):
                def body(i, u):
                    g = 2 * i + u
                    sp.wait_ge(sem("ln_h"), k * GROUPS + g + 1)
                    sp.dma_start(tab[k][bass.ds(g * GN, GN), :].rearrange("(b p) f -> p b f", p=P),
                                 stage[:, u, 0, :].rearrange("p (b f) -> p b f", f=D)).then_inc(sem(f"group_stored{u}"), 16)
                group_loop(sp, body)

            store_h(0)
            sp.wait_ge(sem("asrow_done"), GROUPS)
            load(logit_tab, asrow.rearrange("o (h l) -> o h l", l=LO), "logits_loaded")
            sp.wait_ge(sem("hi_stored"), 16)
            sp.wait_ge(sem("ln0_mm"), GROUPS)
            for u in range(2):
                sp.wait_ge(sem(f"group_stored{u}"), 16 * GROUPS // 2)

            def hi_chunk(i, s):
                src = hi_d[bass.ds((5 * i + s) * 640, 640)].rearrange("(o e) -> o e", o=1).to_broadcast([HI, 640])
                sp.dma_start(hi_bc[:, s, :], src).then_inc(sem(f"hi_loaded{s}"), 16)
            for s in range(5):
                hi_chunk(0, s)
            with sp.Fori(1, 25) as i:
                for s in range(5):
                    sp.wait_ge(sem("hot_made"), 5 * i + s - 4)
                    hi_chunk(i, s)

            sp.wait_ge(sem("zero_made"), 1)
            sp.wait_ge(sem("w_loaded"), 16 * 28)
            for n in range(2 * HALF):
                row = zeros[:, :] if n else att[:, 3, :]
                sp.dma_start(part_d[n].rearrange("(p b) f -> p b f", p=P), row.unsqueeze(1).to_broadcast([P, BLOCKS + 1, D])) \
                    .then_inc(sem("parts_zeroed"), 16)

            def support(i, u):
                g = 2 * i + u
                sp.wait_ge(sem("e1_out"), g + 1)
                sp.dma_start(tab[1][bass.ds(g * GN, GN), :].rearrange("(b p) f -> p b f", p=P),
                             outst[:, u, 0:GN].rearrange("p (b f) -> p b f", f=D)).then_inc(sem(f"group_stored{u}"), 16)
            group_loop(sp, support)
            km = rounds(sp)
            regs = window_regs(sp, "sp")
            for u in range(2):
                sp.wait_ge(sem(f"group_stored{u}"), 2 * 16 * GROUPS // 2)
            sp.wait_ge(sem("src_col"), 1)
            with sp.Fori(0, km) as k:
                sp.wait_ge(sem("round"), (km * 3 + 1) * ROUNDS.index("p1") + k * 3 + 4)
                sp.sem_inc(sem("turn"), 1)
                kk = sp.snap(km + k)

                def half(q, h, done, sources_used):
                    first = windows(sp, regs, five(q))
                    if sources_used is not None:
                        sp.wait_ge(sem("idx_ready"), sources_used)
                        sp.sem_inc(sem("turn"), 1)
                    src = a["src"][bass.ds(q * HALF * P, HALF * P)].rearrange("(o e) -> o e", o=1).to_broadcast([P, HALF * P])
                    sp.dma_start(src_bc[:, h, :], src).then_inc(sem(f"src_bc{h}"), 16)
                    sp.wait_ge(sem("mm_done"), done)
                    sp.sem_inc(sem("turn"), 1)
                    for j in range(HALF):
                        s = h * HALF + j
                        sp.dma_start(ring[0:WIN, s, D:2 * D], tab[1][bass.ds(first[j], WIN), :]).then_inc(sem(f"window{h}"), 16)
                half(0, 0, kk * T + 1, None)
                half(1, 1, kk * T + 1, None)
                with sp.Fori(1, T // (2 * HALF)) as r:
                    for h in range(2):
                        q = 2 * r + h
                        half(q, h, kk * T + (q - 1) * HALF + 1, kk * (T // HALF) + q - 1)
                half(T // HALF - 1, 0, (kk + 1) * T - 2 * HALF + 1, (kk + 1) * (T // HALF) - 2)
                sp.wait_ge(sem("idx_ready"), (kk + 1) * (T // HALF))
                sp.sem_inc(sem("turn"), 1)
            sp.wait_ge(sem("scat0"), km * (80 * 63))
            sp.sem_inc(sem("turn"), 1)
            sp.wait_ge(sem("scat1"), km * (80 * 62))
            sp.sem_inc(sem("turn"), 1)

            def parts(i, u):
                if later(i):
                    sp.wait_ge(sem("parts_added"), (2 * i + u - 1) * HALF)
                    sp.sem_inc(sem("turn"), 1)
                for n in range(HALF):
                    sp.dma_start(parts_in[:, u, n, :].rearrange("p (b f) -> p b f", f=D),
                                 part_d[u * HALF + n][0:NP, :].rearrange("(p b) f -> p b f", p=P)[:, bass.ds(i * 4, 4), :]).then_inc(sem(f"parts_in{u}"), 16)
            for u in range(2):
                parts(0, u)
            with sp.Fori(1, GROUPS) as i:
                for u in range(2):
                    parts(i, u)
            store_h(2)
            def e3(i, u):
                g = 2 * i + u
                for j in range(2):
                    sp.wait_ge(sem("e3_out"), 2 * g + j + 1)
                    sp.dma_start(tab[3][bass.ds(g * GN + 2 * j * P, 2 * P), :].rearrange("(b p) f -> p b f", p=P),
                                 outst[:, j, 0:512].rearrange("p (b f) -> p b f", f=HID)).then_inc(sem(f"e3_stored{j}"), 16)
            group_loop(sp, e3)
            def e4(i, u):
                g = 2 * i + u
                sp.wait_ge(sem("e4_out"), g + 1)
                sp.dma_start(tab[4][bass.ds(g * GN, GN), :].rearrange("(b p) f -> p b f", p=P),
                             outst[:, u, 0:GN].rearrange("p (b f) -> p b f", f=D)).then_inc(sem(f"group_stored{u}"), 16)
            group_loop(sp, e4)
            with sp.Fori(0, km) as k:
                sp.wait_ge(sem("round"), (km * 3 + 1) * ROUNDS.index("p4") + k * 3 + 4)
                sp.sem_inc(sem("turn"), 1)

                def types(q, h, used):
                    if used is not None:
                        sp.wait_ge(sem("toht_made"), used)
                        sp.sem_inc(sem("turn"), 1)
                    sp.dma_start(typ_bc[:, h, :], a["edge_type_8"][bass.ds(q * HALF * P, HALF * P)].rearrange("(o e) -> o e", o=1)
                                 .to_broadcast([RELS, HALF * P])).then_inc(sem(f"typ_in{h}"), 16)
                types(0, 0, None)
                types(1, 1, None)
                with sp.Fori(1, T // (2 * HALF)) as r:
                    for h in range(2):
                        types(2 * r + h, h, k * (T // HALF) + 2 * r + h - 1)
                types(T // HALF - 1, 0, (k + 1) * (T // HALF) - 2)
                sp.wait_ge(sem("toht_made"), (k + 1) * (T // HALF))
                sp.sem_inc(sem("turn"), 1)

            def relation_table(p, weight):
                kc, halves, width = FIRST_TABLES[p]
                for c in range(kc):
                    load(relw[:, c * width:(c + 1) * width].rearrange("p (r o) -> p r o", r=RELS),
                         weight[:, c * P:(c + 1) * P, :].rearrange("r f o -> f r o"), "relw_loaded")
                rows = tab[p].rearrange("(n h) f -> n (h f)", n=NP)

                def body(i, u):
                    g = 2 * i + u
                    per = 4 * halves
                    for j in range(per):
                        sp.wait_ge(sem("unit_outa"), UNITS[p] + g * per + j + 1)
                        sp.wait_ge(sem("unit_outd"), UNITS[p] + g * per + j + 1)
                        b, h = j // halves, j % halves
                        sp.dma_start(rows[bass.ds(g * GN + b * P, P), h * 1024:(h + 1) * 1024].rearrange("p (k n) -> p k n", k=2),
                                     unit_slot(p, j)).then_inc(sem(f"unit_stored{j % 4}"), 16)
                group_loop(sp, body)

            sp.wait_ge(sem("pass_end"), 5)
            relation_table(5, a["L3_gnn_W1"])
            relation_table(6, a["L3_gnn_W2"])
            relation_table(7, a["L3_gnn_W3"])
            sp.wait_ge(sem("x_final"), 1)
            sp.dma_start(out[0:full * P, :].rearrange("(b p) f -> p b f", p=P),
                         X[:, 0:full * P].rearrange("p (b f) -> p b f", f=D)).then_inc(sem("stored"), 16)
            sp.dma_start(out[full * P:N, :], X[0:N - full * P, full * P:NP]).then_inc(sem("stored"), 16)
            sp.wait_ge(sem("stored"), 32)

        @block.gpsimd
        def _(pool):
            pool.memset(X[:, (BLOCKS - 1) * P:NP], 0.0).then_inc(sem("x_padded"), 1)
            pool.memset(BASEF[:, :], 0.0).then_inc(sem("x_padded"), 1)
            pool.memset(ident[:, :], 0.0).then_inc(sem("ident0"), 1)
            spare_rows = spare[:, :]
            for v, pat, mul in ((iotaW[:, :], [[1, WIN]], 0), (iotaL[:, :], [[1, LO]], 0),
                                (iotaR[:, :], [[1, RELS]], 0), (part[:, :], [[0, 1]], 1), (spare_rows, [[0, 1]], 1), (minus_part[:, :], [[0, 1]], -1)):
                pool.iota(v, pat, base=NP if v is spare_rows else 0, channel_multiplier=mul, allow_small_or_imprecise_dtypes=True).then_inc(sem("const"), 1)
            pool.memset(ones[:, :], 1.0).then_inc(sem("const"), 1)
            pool.memset(zeros[:, :], 0.0).then_inc(sem("zero_made"), 1)
            pool.memset(before[:, :], 0.0).then_inc(sem("ident0"), 1)
            pool.wait_ge(sem("ident0"), 2)
            pool.affine_select(out=before[:, :], in_=before[:, :], compare_op=ALU.is_ge, fill=1.0, base=0,
                               pattern=[[1, P]], channel_multiplier=-1).then_inc(sem("const"), 1)
            pool.affine_select(out=ident[:, :], in_=ident[:, :], compare_op=ALU.not_equal, fill=1.0, base=0,
                               pattern=[[-1, P]], channel_multiplier=1).then_inc(sem("const"), 1)

            km = rounds(pool)

            regs = window_regs(pool, "pool", BATCH // 2)

            def lookup(tag, table):
                total = TP // BATCH
                with pool.Fori(0, km) as k:
                    start = pool.snap((km * (tag != "adst") + k) * total)

                    def step(q, s):
                        pool.wait_ge(sem("lookup_hit"), start + q + 1)
                        pool.sem_inc(sem("turn"), 1)
                        bases = windows(pool, regs, BASE16[0:1, bass.ds(q * BATCH + BATCH // 2, BATCH // 2)])
                        for j in range(BATCH // 2):
                            v = place[:, s, BATCH // 2 + j, :]
                            ins = pool.tensor_tensor(v, v, table[:, bass.ds(bases[j], WIN)], ALU.mult)
                        ins.then_inc(sem("lookup_product2"), 1)
                    with pool.Fori(0, total // 2) as i:
                        for s in range(2):
                            step(2 * i + s, s)
            lookup("adst", adstB)
            lookup("max_edge", maxB)

            def gather(p):
                width = PASS[p]["F"]
                for s, n in table_ready(p):
                    pool.wait_ge(s, n)
                with pool.Fori(0, km) as k:
                    kk = pool.snap(km * p + k)

                    def half(q, h):
                        pool.wait_ge(sem("idx_ready"), kk * (T // HALF) + q + 1)
                        pool.sem_inc(sem("turn"), 1)
                        for j in range(HALF):
                            s = h * HALF + j
                            pool.indirect_dma_start(ring[:, s, 0:width], None, tab[p][:, :],
                                                    bass.IndirectOffsetOnAxis(cur[:, s:s + 1], 0)).then_inc(sem(f"row{s}"), 16)
                    with pool.Fori(0, T // (2 * HALF)) as r:
                        for h in range(2):
                            half(2 * r + h, h)
                    half(T // HALF - 1, 0)

            def scatter():
                pool.wait_ge(sem("parts_zeroed"), 16 * 2 * HALF)
                with pool.Fori(0, km) as k:
                    kk = pool.snap(km + k)

                    def half(q, h):
                        pool.wait_ge(sem("idx_ready"), kk * (T // HALF) + q + 1)
                        pool.sem_inc(sem("turn"), 1)
                        pool.wait_ge(sem("psum_free"), kk * T + (q + 1) * HALF + 5)
                        pool.sem_inc(sem("turn"), 1)
                        for j in range(HALF):
                            s = h * HALF + j
                            pool.indirect_dma_start(part_d[s][:, :], bass.IndirectOffsetOnAxis(cur[:, s:s + 1], 0), ring[:, s, 0:D], None,
                                                    compute_op=ALU.add).then_inc(sem(f"scat{h}"), 16)
                    with pool.Fori(0, T // (2 * HALF)) as r:
                        for h in range(2):
                            half(2 * r + h, h)
                    half(T // HALF - 1, 0)

            for p in range(len(PASS)):
                scatter() if p == 1 else gather(p)

        @block.scalar
        def _(act):
            act.wait_ge(sem("watt_made"), 3)
            nc.scalar.copy(wdst[:, :], watt[:, 1:2].to_broadcast([P, P])).then_inc(sem("wdst_made"), 1)
            nc.scalar.copy(vB[:, :], small[0:EDIM, 0:1].to_broadcast([EDIM, P])).then_inc(sem("vB_made"), 1)

            def norm_start(k):
                act.wait_ge(sem("ln_var"), k + 1)
                nc.scalar.activation(std[:, :], std[:, :], ACT.Sqrt).then_inc(sem("ln_std"), 1)
                act.wait_ge(sem("ln_shift"), k + 1)

            def norm_group(k, i, u):
                g = 2 * i + u
                if later(i):
                    if k in (0, 2):
                        act.wait_ge(sem(f"group_stored{u}"), 16 * (STORED[k] * GROUPS // 2 + i))
                    act.wait_ge(sem("ln_tr"), k * GROUPS + g - 1)
                for q in range(4):
                    ins = nc.scalar.activation(stage[:, u, 0, q * P:(q + 1) * P], cols(X, 4 * g + q, P), ACT.Relu,
                                               bias=cols(shift, 4 * g + q, 1), scale=cols(rstd, 4 * g + q, 1))
                ins.then_inc(sem("ln_h"), 1)

            def indices(p):
                idx = PASS[p]["idx"]
                with act.Fori(0, km) as k:
                    kk = act.snap(km * p + k)

                    def half(q, h, done):
                        act.wait_ge(sem("mm_done"), kk * T + done + 1)
                        nc.scalar.copy(cur[:, h * HALF:(h + 1) * HALF], cols(idx, q, HALF)).then_inc(sem("idx_ready"), 1)

                    half(0, 0, 0)
                    half(1, 1, 0)
                    with act.Fori(1, T // (2 * HALF)) as r:
                        for h in range(2):
                            half(2 * r + h, h, (2 * r + h - 1) * HALF)
                    half(T // HALF - 1, 0, T - 2 * HALF)

            def bias_rows(name, dst, bank_of, b, i, u, halves=2):
                g = 2 * i + u
                act.wait_ge(sem(name + "_root"), g + 1)
                for o in range(halves):
                    ins = nc.scalar.activation(dst[:, o, bass.ds(g * GN, GN)], PS[:, bank_of(o), :], ACT.Identity,
                                               bias=bcol[:, b, o:o + 1])
                ins.then_inc(sem(name + "_rooted"), 1)

            def unit_out(p, i, u, j):
                per = 4 * FIRST_TABLES[p][1]
                g = 2 * i + u
                act.wait_ge(sem("unit"), UNITS[p] + g * per + j + 1)
                if later(i) or u or j >= 4:
                    act.wait_ge(sem(f"unit_stored{j % 4}"), 16 * (UNITS[p] // 4 + g * (per // 4) + j // 4))
                nc.scalar.copy(unit_slot(p, j)[:, 0, :], PS[:, 2 * (j % 2), :]).then_inc(sem("unit_outa"), 1)

            def l0(i, u):
                g = 2 * i + u
                act.wait_ge(sem("ln0_mm"), g + 1)
                nc.scalar.copy(asrow[:, bass.ds(g * GN, GN)], PS[0:1, u, :]).then_inc(sem("asrow_done"), 1)
            act.wait_ge(sem("cols_done"), 10)
            act.wait_ge(sem("wT_done"), 7)
            norm_start(0)
            ahead_loop(act, lambda i, u: norm_group(0, i, u), l0)

            def distance(i, s):
                act.wait_ge(sem(f"hi_loaded{s}"), 16 * (i + 1))
                act.sem_inc(sem("turn"), 1)
                if later(i):
                    act.wait_ge(sem("src_mm"), 5 * i + s - 4)
                    act.sem_inc(sem("turn"), 1)
                nc.scalar.activation(hot_hi[:, s, :], hi_bc[:, s, :], ACT.Abs, bias=minus_part[0:HI, :]).then_inc(sem("hot_abs"), 1)

            def hot(i, s):
                act.wait_ge(sem("hot_abs"), 5 * i + s + 1)
                nc.scalar.activation(hot_hi[:, s, :], hot_hi[:, s, :], ACT.Relu, bias=ones[0:HI, 0:1], scale=-1.0).then_inc(sem("hot_made"), 1)

            def hots(i):
                for s in range(5):
                    distance(i, s)
                    if s:
                        hot(i, s - 1)
                hot(i, 4)
            act.wait_ge(sem("const"), 9)
            hots(0)
            with act.Fori(1, 25) as i:
                hots(i)
            km = rounds(act)
            with act.Fori(0, km) as k:
                def spread(g, s):
                    n = k * (TP // BATCH) + g
                    act.wait_ge(sem("mx_red"), n + 1)
                    act.sem_inc(sem("turn"), 1)
                    for q in range(4):
                        ins = nc.scalar.mul(diag[:, s, q * P:(q + 1) * P], ident[:, :], small[:, 4 + 4 * s + q:5 + 4 * s + q])
                    ins.then_inc(sem("mx_diag"), 1)
                with act.Fori(0, TP // BATCH // 2) as i:
                    for s in range(2):
                        spread(2 * i + s, s)
            act.wait_ge(sem("exp_in"), 1)
            nc.scalar.activation(WGT[:, :], WGT[:, :], ACT.Exp).then_inc(sem("wgt_made"), 1)
            act.sem_inc(sem("mm_done"), 1)
            indices(0)
            norm_start(1)

            def l1(i, u):
                act.wait_ge(sem("e1_tab"), 2 * i + u + 1)
                if later(i):
                    act.wait_ge(sem(f"group_stored{u}"), 16 * (STORED[1] * GROUPS // 2 + i))
                nc.scalar.copy(outst[:, u, 0:512], PS[:, 2 + u, :]).then_inc(sem("e1_out"), 1)
            ahead_loop(act, lambda i, u: norm_group(1, i, u), l1)
            with act.Fori(0, km) as k:
                kk = act.snap(km + k)

                def spread_copy(t, s):
                    act.wait_ge(sem("b_mm"), k * T + t + 1)
                    nc.scalar.copy(spread_t[:, s, :], PS[0:WIN, s, 0:P]).then_inc(sem("b_ready"), 1)

                def rows_copy(t, slot):
                    act.wait_ge(sem("mm_done"), kk * T + t + 2)
                    nc.scalar.copy(ring[:, slot, 0:D], PS[:, slot % 5, P:2 * P]).then_inc(sem("psum_free"), 1)

                def half(q, h, landed, last=False):
                    if landed is not None:
                        act.wait_ge(sem(f"scat{h}"), landed)
                    for j in range(HALF):
                        if not (last and j == HALF - 1):
                            spread_copy(q * HALF + j + 1, (j + 1) % 5)
                        rows_copy(q * HALF + j, h * HALF + j)
                spread_copy(0, 0)
                half(0, 0, None)
                half(1, 1, None)
                with act.Fori(1, T // (2 * HALF)) as r:
                    for h in range(2):
                        half(2 * r + h, h, (k * (T // 10 + (h == 0)) + r) * 80)
                half(T // HALF - 1, 0, (k * (T // 10 + 1) + T // 10) * 80, True)
                act.wait_ge(sem("scat0"), (k + 1) * (80 * 63))
                act.wait_ge(sem("scat1"), (k + 1) * (80 * 62))
                act.sem_inc(sem("turn"), 1)
            norm_start(2)

            ahead_loop(act, lambda i, u: norm_group(2, i, u),
                       lambda i, u: bias_rows("ln2", ACC_B, lambda o: 2 * u + o, 0, i, u))
            indices(2)
            def e3_hidden(i, u):
                act.wait_ge(sem("e3_pre"), 2 * i + u + 1)
                nc.scalar.activation(stage2[:, u, :, :], stage2[:, u, :, :], ACT.Relu).then_inc(sem("e3_hid"), 1)

            def e3(i, u):
                g = 2 * i + u
                for j in range(2):
                    act.wait_ge(sem("e3_tr"), 2 * g + j + 1)
                    if later(i) or u:
                        act.wait_ge(sem(f"e3_stored{j}"), 16 * g)
                    nc.scalar.copy(outst[:, j, 0:512], PS[:, 5 + j, :]).then_inc(sem("e3_out"), 1)
            ahead_loop(act, e3_hidden, e3)
            indices(3)
            def e4_hidden(i, u):
                g = 2 * i + u
                act.wait_ge(sem("e4_pre"), g + 1)
                nc.scalar.activation(stage2[:, u, :, :], stage2[:, u, :, :], ACT.Relu).then_inc(sem("e4_hid"), 1)
                nc.scalar.copy(cols(rdeg, g), outst[:, u, 512:1024]).then_inc(sem("rdeg_kept"), 1)

            def e4(i, u):
                g = 2 * i + u
                act.wait_ge(sem("x_mm"), X_PRODUCTS["e4"] * GROUPS + g + 1)
                if later(i):
                    act.wait_ge(sem(f"group_stored{u}"), 16 * (STORED[4] * GROUPS // 2 + i))
                nc.scalar.copy(outst[:, u, 0:512].rearrange("p (q f) -> p q f", f=D), e4_out[:, :, 0:D]).then_inc(sem("e4_out"), 1)
            ahead_loop(act, e4_hidden, e4)
            indices(4)
            norm_start(3)

            def t5(i, u):
                bias_rows("t5", ACC_A, lambda o: 4 + 3 * o, 2, i, u)
                for j in range(8):
                    unit_out(5, i, u, j)
            ahead_loop(act, lambda i, u: norm_group(3, i, u), t5)
            indices(5)

            def hidden_group(p, acc, i, u):
                g = 2 * i + u
                act.wait_ge(sem("pass_end"), p)
                if later(i):
                    act.wait_ge(sem("unit"), UNITS[p] + (g - 1) * 4 * FIRST_TABLES[p][1])
                    act.wait_ge(sem(f"t{p}_root"), g - 1)
                nc.scalar.activation(stage2[:, u, :, :], cols2(acc, g), ACT.Relu).then_inc(sem(f"t{p}_hid"), 1)

            def t6(i, u):
                bias_rows("t6", ACC_B, lambda o: 4 + 3 * o, 3, i, u)
                for j in range(8):
                    unit_out(6, i, u, j)
            ahead_loop(act, lambda i, u: hidden_group(6, ACC_A, i, u), t6)
            indices(6)
            def t7(i, u):
                bias_rows("t7", ACC_A, lambda o: 4, 4, i, u, 1)
                for j in range(4):
                    unit_out(7, i, u, j)
            ahead_loop(act, lambda i, u: hidden_group(7, ACC_B, i, u), t7)
            indices(7)
            def copy_sums(name, i, u):
                g = 2 * i + u
                if later(i):
                    act.wait_ge(sem("x_mm"), X_PRODUCTS[name] * GROUPS + g - 1)
                act.wait_ge(sem("pass_end"), len(PASS))
                nc.scalar.copy(stage[:, u, 0, :], cols(ACC_A[:, 0, :], g)).then_inc(sem(name + "_stage"), 1)
            group_loop(act, lambda i, u: copy_sums("e8", i, u))


        @block.vector
        def _(dve):
            vec = nc.vector
            link = Chain(dve, "dve_step")

            dve.wait_ge(sem("const"), 9)
            vec.memset(REL[:, :], -1.0).then_inc(sem("cleared"), 1)
            vec.memset(TYP[:, :], 0.0).then_inc(sem("cleared"), 1)
            vec.memset(EWT[:, :], 0.0).then_inc(sem("cleared"), 1)
            vec.memset(MULTI[:, 0:6 * TP], 0.0).then_inc(sem("cleared"), 1)
            dve.wait_ge(sem("rows_loaded"), 64)
            vec.tensor_copy(dst_f, dst_r).then_inc(sem("dst_f"), 1)
            vec.tensor_copy(src_f, src_r).then_inc(sem("rows_made"), 1)
            vec.tensor_copy(typ_f, typ_r).then_inc(sem("rows_made"), 1)
            link(vec.tensor_scalar(hi_i, src_r, LO.bit_length() - 1, None, ALU.arith_shift_right))
            vec.tensor_copy(hi_b, hi_i).then_inc(sem("hi_made"), 1)
            dve.wait_ge(sem("dst_f"), 1)
            vec.tensor_reduce(high_f, dst_f, AX, ALU.max).then_inc(sem("dst_f"), 1)
            vec.tensor_reduce(base_f, dst_f, AX, ALU.min).then_inc(sem("base_made"), 1)
            dve.wait_ge(sem("base_made"), 1)
            dve.wait_ge(sem("dst_f"), 2)
            vec.tensor_tensor(rel_f, dst_f, base_f.unsqueeze(2).to_broadcast([RQ, RB, P]), ALU.subtract).then_inc(sem("rows_made"), 1)
            link(vec.tensor_tensor(high_f, high_f, base_f, ALU.subtract))
            vec.tensor_reduce(span_f, high_f, AX, ALU.max).then_inc(sem("rows_made"), 1)
            dve.wait_ge(sem("cleared"), 4)
            for n, v in enumerate((SRC, TYP, REL, EWT)):
                dve.wait_ge(sem("rows_tr"), n + 1)
                vec.tensor_copy(v[:, 0:500], PS[:, 2 * n, 0:500]).then_inc(sem("cols_done"), 1)
                vec.tensor_copy(v[:, 500:T], PS[:, 2 * n + 1, 0:T - 500]).then_inc(sem("cols_done"), 1)
            dve.wait_ge(sem("cols_done"), 8)
            vec.scalar_tensor_tensor(KEY[:, 0:500], PS[:, 0, 0:500], float(RELS), TYP[:, 0:500], ALU.mult, ALU.add).then_inc(sem("cols_done"), 1)
            vec.scalar_tensor_tensor(KEY[:, 500:T], PS[:, 1, 0:T - 500], float(RELS), TYP[:, 500:T], ALU.mult, ALU.add).then_inc(sem("cols_done"), 1)
            low = ALPHA.bitcast(I32)[:, 0:T]
            link(vec.tensor_scalar(low, SRC[:, 0:T], LO - 1, None, ALU.bitwise_and))
            link(vec.tensor_copy(SLO[:, 0:T], low))
            link(vec.memset(ALPHA, 0.0))

            dve.wait_ge(sem("w_loaded"), 16 * 28)
            junk = outst[:, 0, 0:D]
            link(vec.scalar_tensor_tensor(junk, W0[:, :], 1.0, att[:, 0, :], ALU.mult, ALU.mult, accum_out=watt[:, 0:1]))
            dve.sem_inc(sem("watt_made"), 1)
            link(vec.scalar_tensor_tensor(junk, W0[:, :], 1.0, att[:, 1, :], ALU.mult, ALU.mult, accum_out=watt[:, 1:2]))
            dve.sem_inc(sem("watt_made"), 1)
            link(vec.scalar_tensor_tensor(junk[0:EDIM, :], we_sb[:, :], 1.0, att[0:EDIM, 2, :], ALU.mult, ALU.mult, accum_out=small[0:EDIM, 0:1]))
            dve.sem_inc(sem("watt_made"), 1)
            dve.wait_ge(sem("wT_tr"), 1)
            at = 0
            for w, oc, fc in ((Wl1T, 2, 1), (Wr1T, 2, 1), (Wl2T, 2, 2), (Wr2T, 2, 2), (W3T[:, :, 0:D], 1, 2), (W3T[:, :, D:2 * D], 1, 2), (None, 1, 2)):
                if w is None:
                    dve.wait_ge(sem("wT_done"), 6)
                for o in range(oc):
                    for c in range(fc):
                        block_in = PS[:, at // 4, (at % 4) * P:(at % 4 + 1) * P]
                        at += 1
                        if w is None:
                            v = W3T[:, c, D:2 * D]
                            ins = vec.tensor_tensor(v, v, block_in, ALU.add)
                            continue
                        dst = w[:, o * P:(o + 1) * P] if fc == 1 else w[:, c, o * P:(o + 1) * P]
                        ins = vec.tensor_copy(dst, block_in)
                ins.then_inc(sem("wT_done"), 1)
            dve.wait_ge(sem("span_tr"), 1)
            link(vec.tensor_reduce(small[0:1, 2:3], PS[0:1, 5, 0:RQ], AX, ALU.max))
            link(vec.tensor_copy(spans[:, :], small[0:1, 2:3]))
            link(vec.tensor_scalar(spans[:, :], spans[:, :], WIN_SHIFT, None, ALU.arith_shift_right))
            link(vec.tensor_scalar(spans[:, :], spans[:, :], 1.0, None, ALU.add))
            dve.sem_inc(sem("spans_known"), 5)

            dve.wait_ge(sem("vrow_mm"), 1)
            link(vec.tensor_copy(vrow[:, :], PS[:, 6, 0:EDIM]))
            for c in range(5):
                v = ea[c % 2].rearrange("p (j f) -> p j f", f=EDIM)
                dve.wait_ge(sem(f"ea_loaded{c % 2}"), 16 * (c // 2 + 1))
                link(vec.tensor_tensor(v, v, vrow[:, :].unsqueeze(1).to_broadcast([P, 125, EDIM]), ALU.mult))
                link(vec.tensor_reduce(aflat[:, c * 125:(c + 1) * 125], v, AX, ALU.add))
                dve.sem_inc(sem("ea_used"), 1)
                dve.sem_inc(sem("aed_made"), 1)

            def group_stats(k, g):
                c, n = sem("ln_stats"), 3 * GROUPS * k
                if k or later(g):
                    dve.wait_ge(c, n + 3 * g)
                for j in range(4):
                    ins = vec.bn_stats(stats[:, j, :], cols(X, 4 * g + j, P))
                ins.then_inc(c, 1)
                dve.wait_ge(c, n + 3 * g + 1)
                dve.sem_inc(sem("turn"), 1)
                for j in range(4):
                    ins = vec.bn_aggr(group_mv[:, j, :], stats[:, j, :])
                ins.then_inc(c, 1)
                dve.wait_ge(c, n + 3 * g + 2)
                vec.tensor_copy(mv[:, bass.ds(4 * g, 4), :], group_mv[:, :, :]).then_inc(c, 1)

            def norm_scale(k):
                dve.wait_ge(sem("ln_stats"), 3 * GROUPS * (k + 1))
                vec.tensor_scalar(std[:, :], mv[:, :, 1], 1e-5, None, ALU.add).then_inc(sem("ln_var"), 1)
                dve.wait_ge(sem("ln_std"), k + 1)
                link(vec.reciprocal(rstd[:, :], std[:, :]))
                vec.scalar_tensor_tensor(shift[:, :], mv[:, :, 0], -1.0, rstd[:, :], ALU.mult, ALU.mult).then_inc(sem("ln_shift"), 1)

            def transposed_group(k, i, u, used, per):
                g = 2 * i + u
                dve.wait_ge(sem("ln_tr"), k * GROUPS + g + 1)
                if later(i):
                    dve.wait_ge(sem(used), (g - 1) * per)
                vec.tensor_copy(stage2[:, u, 0, :], PS[:, 5 + u, :]).then_inc(sem("ln_ht"), 1)

            def round_start(tag, k):
                s, n = sem("round"), (km * 3 + 1) * ROUNDS.index(tag) + k * 3
                dve.wait_ge(s, n + 1)
                vec.tensor_scalar(iotaK[:, :], iotaW[:, :], koff[:, :], None, ALU.add).then_inc(s, 1)
                if tag in ("adst", "max", "max_edge"):
                    to, bases = BASE16[:, :], BASEF[:, :]
                else:
                    to = BASEK[:, :].rearrange("o (q e) -> o q e", e=8)[:, :, 0:HALF]
                    bases = BASEF[:, :].rearrange("o (q e) -> o q e", e=HALF)
                vec.tensor_scalar(to, bases, koff[0:1, :], float(NP - WIN), ALU.add, ALU.min).then_inc(s, 1)
                dve.wait_ge(s, n + 3)
                vec.tensor_scalar(koff[:, :], koff[:, :], float(WIN), None, ALU.add).then_inc(s, 1)
                dve.wait_ge(s, n + 4)
                dve.sem_inc(sem("turn"), 1)

            def rounds_reset(tag):
                vec.memset(koff[:, :], 0.0).then_inc(sem("round"), 1)

            regs = window_regs(dve, "dve", BATCH)

            dve.wait_ge(sem("x_loaded"), 32)
            dve.wait_ge(sem("x_padded"), 1)
            group_stats(0, 0)
            with dve.Fori(1, GROUPS) as g:
                group_stats(0, g)
            norm_scale(0)

            def l0(i, u):
                g = 2 * i + u
                dve.wait_ge(sem("ln0_mm"), g + 1)
                vec.tensor_copy(cols(adstB, g), PS[:, 2 + u, :]).then_inc(sem("adst_done"), 1)
            ahead_loop(dve, lambda i, u: transposed_group(0, i, u, "ln0_mm", 1), l0)
            dve.wait_ge(sem("aed_tr"), 1)
            link(vec.tensor_copy(AEDG[:, 0:500], PS[:, 5, 0:500]))
            link(vec.tensor_copy(AEDG[:, 500:T], PS[:, 6, 0:T - 500]))

            dve.wait_ge(sem("logits_loaded"), 16)
            rest = logit_tab
            for n in range(3):
                link(vec.tensor_copy(logit_part[:, n, :], rest))
                if n < 2:
                    link(vec.tensor_tensor(logit_rest, rest, logit_part[:, n, :], ALU.subtract))
                    rest = logit_rest
            dve.sem_inc(sem("logits_split"), 1)

            def low_digits(q, s):
                if not isinstance(q, int) or q >= 5:
                    dve.wait_ge(sem("picked"), q - 4)
                vec.tensor_tensor(picks[:, s], iotaL[:, :].unsqueeze(1).to_broadcast([P, 5, LO]),
                                  cols(SLO, q, 5).unsqueeze(2).to_broadcast([P, 5, LO]), ALU.is_equal).then_inc(sem("pick_hot"), 1)

            def products(q, s):
                dve.wait_ge(sem("pick_hot"), q + 1)
                dve.wait_ge(sem("src_mm"), q + 1)
                vec.tensor_tensor(picks[:, s], picks[:, s], PS[:, s, 0:320].rearrange("p (j l) -> p j l", l=LO), ALU.mult).then_inc(sem("pick_mul"), 1)

            def pick(q, s):
                dve.wait_ge(sem("pick_mul"), q + 1)
                vec.tensor_reduce(cols(ASRC, q, 5), picks[:, s], AX, ALU.add).then_inc(sem("picked"), 1)

            low_digits(0, 0)
            for q in range(5):
                low_digits(q + 1, (q + 1) % 5)
                products(q, q)
                if q:
                    pick(q - 1, q - 1)
            with dve.Fori(1, 25) as i:
                for s in range(5):
                    low_digits(5 * i + s + 1, (s + 1) % 5)
                    products(5 * i + s, s)
                    pick(5 * i + s - 1, (s - 1) % 5)
            pick(T // 5 - 1, 4)
            km = rounds(dve)
            dve.wait_ge(sem("base_loaded"), 16)

            def lookup(tag, table, dest):
                rounds_reset(tag)
                total = TP // BATCH
                found = small[:, BATCH:3 * BATCH].rearrange("p (u j) -> p u j", u=2)
                hit, product, summed, added = (sem(f"lookup_{x}") for x in ("hit", "product", "sum", "add"))
                with dve.Fori(0, km) as k:
                    round_start(tag, k)
                    start = dve.snap((km * (tag != "adst") + k) * total)

                    def match(q, s):
                        vec.tensor_tensor(place[:, s], iotaK[:, :].unsqueeze(1).to_broadcast([P, BATCH, WIN]),
                                          cols(REL, q, BATCH).unsqueeze(2).to_broadcast([P, BATCH, WIN]), ALU.is_equal).then_inc(hit, 1)

                    def add(q, s):
                        dve.wait_ge(summed, start + q + 1)
                        vec.tensor_tensor(cols(dest, q, BATCH), cols(dest, q, BATCH), found[:, s], ALU.add).then_inc(added, 1)

                    def step(q, s, first=False, last=False):
                        bases = windows(dve, regs[0:BATCH // 2], BASE16[0:1, bass.ds(q * BATCH, BATCH // 2)])
                        dve.wait_ge(hit, start + q + 1)
                        for j in range(BATCH // 2):
                            v = place[:, s, j, :]
                            ins = vec.tensor_tensor(v, v, table[:, bass.ds(bases[j], WIN)], ALU.mult)
                        ins.then_inc(product, 1)
                        if not first:
                            add(q - 1, 1 - s)
                        if not last:
                            match(q + 1, 1 - s)
                        dve.wait_ge(product, start + q + 1)
                        dve.wait_ge(sem("lookup_product2"), start + q + 1)
                        vec.tensor_reduce(found[:, s], place[:, s], AX, ALU.add).then_inc(summed, 1)
                    match(0, 0)
                    step(0, 0, first=True)
                    step(1, 1)
                    with dve.Fori(1, total // 2 - 1) as i:
                        for s in range(2):
                            step(2 * i + s, s)
                    step(total - 2, 0)
                    step(total - 1, 1, last=True)
                    add(total - 1, 1)
                    dve.wait_ge(added, start + total)
                    dve.sem_inc(sem("turn"), 1)

            lookup("adst", adstB, ADST)
            dve.wait_ge(sem("picked"), T // 5)
            link(vec.tensor_tensor(ALPHA, ASRC, ADST, ALU.add))
            link(vec.tensor_tensor(ALPHA, ALPHA, AEDG, ALU.add))
            link(vec.scalar_tensor_tensor(ALPHA, ALPHA, 0.2, ALPHA, ALU.mult, ALU.max))

            rounds_reset("max")
            for v in maxima:
                vec.memset(v, NEG).then_inc(sem("mx_done"), 1)
            with dve.Fori(0, km) as k:
                round_start("max", k)

                def masked(g, s):
                    n = k * (TP // BATCH) + g
                    v = pen[:, s, :].rearrange("p (j w) -> p j w", w=WIN)
                    vec.tensor_tensor(v, iotaK[:, :].unsqueeze(1).to_broadcast([P, BATCH, WIN]),
                                      cols(REL, g, BATCH).unsqueeze(2).to_broadcast([P, BATCH, WIN]), ALU.not_equal).then_inc(sem("mx_pen"), 1)
                    dve.wait_ge(sem("mx_pen"), n + 1)
                    vec.scalar_tensor_tensor(v, v, NEG, cols(ALPHA, g, BATCH).unsqueeze(2).to_broadcast([P, BATCH, WIN]),
                                             ALU.mult, ALU.add).then_inc(sem("mx_masked"), 1)

                def reduced(g, s):
                    dve.wait_ge(sem("mx_tr"), k * (TP // BATCH) + g + 1)
                    vec.tensor_reduce(small[:, 4 + 4 * s:8 + 4 * s], PS[:, s, :].rearrange("p (a e) -> p a e", e=P), AX, ALU.max).then_inc(sem("mx_red"), 1)

                def merged(g, s):
                    n = k * (TP // BATCH) + g
                    first = windows(dve, regs, BASE16[0:1, bass.ds(BATCH * g, BATCH)])
                    dve.wait_ge(sem("mx_all"), n + 1)
                    for j in range(BATCH):
                        v = maxima[j % 4][:, bass.ds(first[j], WIN)]
                        if j % 4 == 0:
                            dve.wait_ge(sem("mx_done"), n * (BATCH // 4) + j // 4 + 4)
                        ins = vec.tensor_tensor(v, v, PS[:, 2 + s, j * WIN:(j + 1) * WIN], ALU.max)
                        if j % 4 == 3:
                            ins.then_inc(sem("mx_done"), 1)
                masked(0, 0)
                masked(1, 1)
                reduced(0, 0)
                with dve.Fori(1, TP // BATCH // 2) as i:
                    for s in range(2):
                        masked(2 * i + s, s)
                        reduced(2 * i + s - 1, (s - 1) % 2)
                        merged(2 * i + s - 2, s)
                reduced(TP // BATCH - 1, 1)
                merged(TP // BATCH - 2, 0)
                merged(TP // BATCH - 1, 1)
            dve.wait_ge(sem("mx_done"), km * (TP // 4) + 4)
            dve.sem_inc(sem("turn"), 1)
            vec.tensor_tensor(maxima[2], maxima[2], maxima[3], ALU.max)
            link(vec.tensor_tensor(maxB, maxB, maxima[1], ALU.max))
            link(vec.tensor_tensor(maxB, maxB, maxima[2], ALU.max))
            lookup("max_edge", maxB, MAXE)
            vec.tensor_tensor(WGT[:, :], ALPHA, MAXE, ALU.subtract).then_inc(sem("exp_in"), 1)
            dve.wait_ge(sem("wgt_made"), 1)
            dve.sem_inc(sem("psum_free"), 5)

            def sums(p):
                c = PASS[p]
                acc, C = c["acc"], chunks(p)
                if c["zero"]:
                    link(vec.memset(acc[:, 0:C, :], 0.0))
                if c.get("count"):
                    link(vec.memset(cnt8, 0.0))
                if c.get("lookup"):
                    link(vec.memset(WGT[:, :], 0.0))
                rounds_reset(f"p{p}")
                with dve.Fori(0, km) as k:
                    kk = dve.snap(km * p + k)
                    round_start(f"p{p}", k)

                    def select(t, s):
                        col = REL[:, bass.ds(t, 1)]
                        if c["wt"] is None:
                            ins = vec.tensor_scalar(SEL[:, s, :], iotaK[:, :], col, None, ALU.is_equal)
                        else:
                            ins = vec.tensor_scalar(SEL[:, s, :], iotaK[:, :], col, c["wt"][:, bass.ds(t, 1)], ALU.is_equal, ALU.mult)
                        if c.get("count"):
                            ins = vec.tensor_scalar(TOH[:, s, :], iotaR[:, :], TYP[:, bass.ds(t, 1)], None, ALU.is_equal)
                        ins.then_inc(sem("s_ready"), 1)

                    def tile(t, s, q, bases):
                        select(t + AHEAD, (s + AHEAD) % 5)
                        first = bases[s]
                        dve.wait_ge(sem("mm_done"), kk * T + t + 2)
                        dve.wait_ge(sem("psum_free"), kk * T + t + 5)
                        if c.get("count"):
                            v = cnt8[:, bass.ds(first, WIN)]
                            vec.tensor_tensor(v, v, PS[0:RELS, s, 64:64 + WIN], ALU.add)
                        if c.get("lookup"):
                            vec.tensor_tensor(hits[:, s * WIN:(s + 1) * WIN], SEL[:, s, :], PS[:, s, 64:64 + WIN], ALU.mult)
                        v = acc[:, 0:C, bass.ds(first, WIN)]
                        vec.tensor_tensor(v, v, PS[:, s, 0:C * WIN].rearrange("p (c w) -> p c w", w=WIN), ALU.add).then_inc(sem("psum_free"), 1)
                        if c.get("lookup") and s == 4:
                            dve.wait_ge(sem("psum_free"), kk * T + t + 6)
                            vec.tensor_reduce(small[:, 8:13], hits.rearrange("p (j w) -> p j w", w=WIN), AX, ALU.add).then_inc(sem("cnt_edge"), 1)
                            n = k * (T // 5) + q
                            dve.wait_ge(sem("cnt_edge"), n * 2 + 1)
                            vec.tensor_tensor(cols(WGT, q, 5), cols(WGT, q, 5), small[:, 8:13], ALU.add).then_inc(sem("cnt_edge"), 1)
                    def onehots(q, h, use):
                        if c.get("lookup"):
                            dve.wait_ge(sem(f"typ_in{h}"), use * 16)
                            vec.tensor_scalar(TOHT[:, h, :], typ_bc[:, h, :], part[0:RELS, :], None, ALU.is_equal).then_inc(sem("toht_made"), 1)
                    for t in range(AHEAD):
                        select(t, t)
                    onehots(0, 0, k * (T // 10 + 1) + 1)
                    with dve.Fori(0, T // 10) as r:
                        for h in range(2):
                            bases = windows(dve, regs[0:HALF], five(2 * r + h))
                            onehots(2 * r + h + 1, 1 - h, k * (T // 10 + h) + r + 1 + h)
                            for j in range(HALF):
                                tile(10 * r + h * HALF + j, j, 2 * r + h, bases)
                    bases = windows(dve, regs[0:HALF], five(T // HALF - 1))
                    for j in range(HALF):
                        tile(T - HALF + j, j, T // HALF - 1, bases)
                    dve.wait_ge(sem("psum_free"), (kk + 1) * T + 5)
                    dve.sem_inc(sem("turn"), 1)
                dve.sem_inc(sem("pass_end"), 1)

            def sums_by_source():
                rounds_reset("p1")
                dve.wait_ge(sem("e1_tab"), GROUPS)
                vec.tensor_copy(src_col[:, 0:T], SRC[:, 0:T]).then_inc(sem("src_col"), 1)
                link(vec.tensor_scalar(row_low, SRC[:, 0:T], P - 1, None, ALU.bitwise_and))
                link(vec.tensor_scalar(row_high, SRC[:, 0:T], P.bit_length() - 1, None, ALU.arith_shift_right))
                link(vec.scalar_tensor_tensor(row_col, row_low, float(BLOCKS), row_high, ALU.mult, ALU.add))
                with dve.Fori(0, km) as k:
                    kk = dve.snap(km + k)
                    round_start("p1", k)
                    dve.wait_ge(sem("src_col"), 1)

                    def tile(t, s, h, j):
                        if not isinstance(t, int) or t >= 5:
                            dve.wait_ge(sem("b_mm"), k * T + t - 4)
                        vec.tensor_scalar(SEL[:, s, :], iotaK[:, :], REL[:, bass.ds(t, 1)], None, ALU.is_equal)
                        vec.tensor_scalar(same[:, s, :], src_bc[:, h, j * P:(j + 1) * P], src_col[:, bass.ds(t, 1)], EWT[:, bass.ds(t, 1)],
                                          ALU.is_equal, ALU.mult).then_inc(sem("s_ready"), 1)

                    def half(q, h, uses, landed):
                        n = (k * (T // HALF) + q) * (HALF + 4)
                        c = sem("twins")
                        dup, idx = small[:, 8:13], small[:, 3:8]
                        dve.wait_ge(sem(f"src_bc{h}"), uses * 16)
                        for j in range(HALF):
                            vec.scalar_tensor_tensor(twins[:, j, :], src_bc[:, h, j * P:(j + 1) * P], src_col[:, bass.ds(q * HALF + j, 1)],
                                                     before[:, :], ALU.is_equal, ALU.mult).then_inc(c, 1)
                        tile(q * HALF, 0, h, 0)
                        dve.wait_ge(c, n + HALF)
                        vec.tensor_reduce(dup, twins, AX, ALU.add).then_inc(c, 1)
                        vec.tensor_scalar(idx, cols(row_col, q, HALF), -1.0, spare[:, :], ALU.mult, ALU.add).then_inc(c, 1)
                        tile(q * HALF + 1, 1, h, 1)
                        dve.wait_ge(c, n + HALF + 2)
                        vec.scalar_tensor_tensor(idx, dup, 0.5, idx, ALU.is_gt, ALU.mult).then_inc(c, 1)
                        tile(q * HALF + 2, 2, h, 2)
                        dve.wait_ge(c, n + HALF + 3)
                        vec.tensor_tensor(idx, idx, cols(row_col, q, HALF), ALU.add).then_inc(c, 1)
                        tile(q * HALF + 3, 3, h, 3)
                        tile(q * HALF + 4, 4, h, 4)
                        dve.wait_ge(c, n + HALF + 4)
                        if landed is not None:
                            dve.wait_ge(sem(f"scat{h}"), landed)
                        vec.tensor_copy(cur[:, h * HALF:(h + 1) * HALF], idx).then_inc(sem("idx_ready"), 1)
                        dve.wait_ge(sem("idx_ready"), kk * (T // HALF) + q + 1)
                        dve.sem_inc(sem("turn"), 1)
                    half(0, 0, k * (T // 10 + 1) + 1, None)
                    half(1, 1, k * (T // 10) + 1, None)
                    with dve.Fori(1, T // 10) as r:
                        for h in range(2):
                            half(2 * r + h, h, k * (T // 10 + (h == 0)) + r + 1, (k * (T // 10 + (h == 0)) + r) * 80)
                    half(T // HALF - 1, 0, (k + 1) * (T // 10 + 1), (k * (T // 10 + 1) + T // 10) * 80)
                    dve.sem_inc(sem("s_ready"), AHEAD)
                    dve.wait_ge(sem("b_mm"), k * T + T)
                    dve.wait_ge(sem("scat0"), (k + 1) * (80 * 63))
                    dve.wait_ge(sem("scat1"), (k + 1) * (80 * 62))
                    dve.sem_inc(sem("turn"), 1)
                dve.sem_inc(sem("pass_end"), 1)

            def add_x(name, i, u, bank):
                g = 2 * i + u
                dve.wait_ge(sem("x_mm"), X_PRODUCTS[name] * GROUPS + g + 1)
                vec.tensor_tensor(cols(X, g), cols(X, g), PS[:, bank(u), :], ALU.add).then_inc(sem("x_added"), 1)

            def x_done(name):
                dve.wait_ge(sem("x_added"), X_TERMS[name] * GROUPS + GROUPS)

            def mean(name, i, u, C):
                g = 2 * i + u
                r = outst[:, u, 512:1024]
                if name == "e4" and later(i):
                    dve.wait_ge(sem("rdeg_kept"), g - 1)
                dve.wait_ge(sem("deg"), MEANS[name] * GROUPS + g + 1)
                vec.tensor_scalar(r, PS[:, 4, :], 1.0, None, ALU.max).then_inc(sem("deg_max"), 1)
                dve.wait_ge(sem("deg_max"), MEANS[name] * GROUPS + g + 1)
                vec.reciprocal(r, r).then_inc(sem("deg_rec"), 1)
                dve.wait_ge(sem("deg_rec"), MEANS[name] * GROUPS + g + 1)
                if later(i):
                    dve.wait_ge(sem(name + "_mean_mm"), g - 1)
                for ch in range(C):
                    ins = vec.tensor_tensor(stage[:, u, ch, :], cols(ACC_A[:, ch, :], g), r, ALU.mult)
                ins.then_inc(sem(name + "_stage"), 1)

            def hidden_pre(name, i, u):
                g = 2 * i + u
                dve.wait_ge(sem(name + "_mean_mm"), g + 1)
                if later(i):
                    if name == "e4":
                        dve.wait_ge(sem("x_mm"), X_PRODUCTS[name] * GROUPS + g - 1)
                    else:
                        dve.wait_ge(sem(name + "_hid_mm"), g - 1)
                for o in range(2):
                    ins = vec.tensor_tensor(stage2[:, u, o, :], PS[:, 2 * u + o, :], cols(ACC_B[:, o, :], g), ALU.add)
                ins.then_inc(sem(name + "_pre"), 1)

            sums(0)

            def e1(i, u):
                g = 2 * i + u
                den = outst[:, u, 512:1024]
                vec.tensor_scalar(den, cols(ACC_A[:, 1, :], g), 1e-16, None, ALU.add).then_inc(sem("e1_den"), 1)
                dve.wait_ge(sem("e1_den"), g + 1)
                vec.reciprocal(den, den).then_inc(sem("den_rec"), 1)
                dve.wait_ge(sem("den_rec"), g + 1)
                if later(i):
                    dve.wait_ge(sem("x_mm"), X_PRODUCTS["e1"] * GROUPS + g - 1)
                vec.tensor_tensor(stage[:, u, 0, :], cols(ACC_A[:, 0, :], g), den, ALU.mult).then_inc(sem("e1_stage"), 1)
            def add_and_stats(k, name, i, u):
                add_x(name, i, u, lambda u: 5 + u)
                dve.wait_ge(sem("x_added"), X_TERMS[name] * GROUPS + 2 * i + u + 1)
                dve.sem_inc(sem("turn"), 1)
                group_stats(k, 2 * i + u)
            ahead_loop(dve, e1, lambda i, u: add_and_stats(1, "e1", i, u))
            norm_scale(1)
            group_loop(dve, lambda i, u: transposed_group(1, i, u, "e1_tab", 1))
            sums_by_source()
            def add_parts(i, u):
                dve.wait_ge(sem(f"parts_in{u}"), (i + 1) * (16 * HALF))
                for n in range(HALF):
                    if n or u or later(i):
                        dve.wait_ge(sem("parts_added"), (2 * i + u) * HALF + n)
                    ins = vec.tensor_tensor(cols(X, i), cols(X, i), parts_in[:, u, n, :], ALU.add)
                    ins.then_inc(sem("parts_added"), 1)
                if u:
                    dve.wait_ge(sem("parts_added"), (2 * i + u + 1) * HALF)
                    dve.sem_inc(sem("x_added"), 1)
            for u in range(2):
                add_parts(0, u)
            group_stats(2, 0)
            with dve.Fori(1, GROUPS) as i:
                for u in range(2):
                    add_parts(i, u)
                group_stats(2, i)
            norm_scale(2)
            group_loop(dve, lambda i, u: transposed_group(2, i, u, "ln2_root", 1))
            sums(2)
            def e3(i, u):
                g = 2 * i + u
                dve.wait_ge(sem("e3_hid_mm"), g + 1)
                for o in range(2):
                    v = cols(ACC_B[:, o, :], g)
                    ins = vec.scalar_tensor_tensor(v, PS[:, 2 * u + o, :], bcol[:, 1, o:o + 1], stage2[:, u, o, :], ALU.add, ALU.add)
                ins.then_inc(sem("e3_root"), 1)

            def e3_hidden(i, u):
                hidden_pre("e3", i, u)
                if following(i, u):
                    mean("e3", *following(i, u), 1)
            mean("e3", 0, 0, 1)
            ahead_loop(dve, e3_hidden, e3)
            dve.wait_ge(sem("e3_root"), GROUPS)
            sums(3)
            def e4(i, u):
                g = 2 * i + u
                dve.wait_ge(sem("e4_out"), g + 1)
                v = cols(X, g).rearrange("p (q f) -> p q f", f=D)
                vec.tensor_tensor(v, v, e4_out[:, :, D:2 * D], ALU.add).then_inc(sem("x_added"), 1)

            def e4_hidden(i, u):
                hidden_pre("e4", i, u)
                if following(i, u):
                    mean("e4", *following(i, u), 2)
            mean("e4", 0, 0, 2)
            ahead_loop(dve, e4_hidden, e4)
            x_done("e4")
            sums(4)
            dve.wait_ge(sem("cnt_edge"), km * (2 * (T // 5)))
            link(vec.tensor_scalar(WGT[:, :], WGT[:, :], 1.0, None, ALU.max))
            link(vec.reciprocal(WGT[:, :], WGT[:, :]))

            def e5(i, u):
                g = 2 * i + u
                if later(i):
                    dve.wait_ge(sem("x_mm"), X_PRODUCTS["e5"] * GROUPS + g - 1)
                vec.tensor_tensor(stage[:, u, 0, :], cols(ACC_A[:, 0, :], g), cols(rdeg, g), ALU.mult).then_inc(sem("e5_stage"), 1)
            dve.wait_ge(sem("rdeg_kept"), GROUPS)
            ahead_loop(dve, e5, lambda i, u: add_and_stats(3, "e5", i, u))
            norm_scale(3)

            def unit_out(p, i, u, j):
                g = 2 * i + u
                per = 4 * FIRST_TABLES[p][1]
                dve.wait_ge(sem("unit"), UNITS[p] + g * per + j + 1)
                if later(i) or u or j >= 4:
                    dve.wait_ge(sem(f"unit_stored{j % 4}"), 16 * (UNITS[p] // 4 + g * (per // 4) + j // 4))
                vec.tensor_copy(unit_slot(p, j)[:, 1, :], PS[:, 2 * (j % 2) + 1, :]).then_inc(sem("unit_outd"), 1)

            def t5(i, u):
                for j in range(8):
                    unit_out(5, i, u, j)
            ahead_loop(dve, lambda i, u: transposed_group(3, i, u, "unit", 8), t5)
            sums(5)
            def t6(i, u):
                for j in range(8):
                    unit_out(6, i, u, j)
            group_loop(dve, t6)
            sums(6)
            def t7(i, u):
                for j in range(4):
                    unit_out(7, i, u, j)
            group_loop(dve, t7)
            sums(7)
            group_loop(dve, lambda i, u: add_x("e8", i, u, lambda u: 5 + u))
            x_done("e8")
            dve.sem_inc(sem("x_final"), 1)

        @block.tensor
        def _(pe):
            mm = nc.tensor.matmul

            pe.wait_ge(sem("const"), 9)
            pe.wait_ge(sem("rows_loaded"), 64)
            pe.wait_ge(sem("rows_made"), 4)
            for n, v in enumerate((src_f, typ_f, rel_f, ewt_r)):
                for b in range(RB):
                    ins = nc.tensor.transpose(PS[:, 2 * n + b // 4, (b % 4) * RQ:(b % 4 + 1) * RQ], v[:, b, :], ident[0:RQ, 0:RQ])
                ins.then_inc(sem("rows_tr"), 1)
            pe.wait_ge(sem("cols_done"), 10)
            pe.wait_ge(sem("w_loaded"), 16 * 28)
            for n in range(18):
                ins = nc.tensor.transpose(PS[:, n // 4, (n % 4) * P:(n % 4 + 1) * P], wraw[:, n, :], ident[:, :])
            ins.then_inc(sem("wT_tr"), 1)
            nc.tensor.transpose(PS[0:1, 5, 0:RQ], span_f, ident[0:RQ, 0:RQ]).then_inc(sem("span_tr"), 1)
            pe.wait_ge(sem("vB_made"), 1)
            mm(PS[:, 6, 0:EDIM], vB[:, :], ident[0:EDIM, 0:EDIM], start=True, stop=True).then_inc(sem("vrow_mm"), 1)

            def transpose_group(k, i, u):
                g = 2 * i + u
                pe.wait_ge(sem("ln_h"), k * GROUPS + g + 1)
                if later(i):
                    pe.wait_ge(sem("ln_ht"), k * GROUPS + g - 1)
                for q in range(4):
                    ins = nc.tensor.transpose(PS[:, 5 + u, q * P:(q + 1) * P], stage[:, u, 0, q * P:(q + 1) * P], ident[:, :])
                ins.then_inc(sem("ln_tr"), 1)

            def transposed(k, i, u):
                pe.wait_ge(sem("ln_ht"), k * GROUPS + 2 * i + u + 1)

            pe.wait_ge(sem("wdst_made"), 1)
            pe.wait_ge(sem("spans_known"), 1)
            pe.wait_ge(sem("ea_used"), 1)
            pe.wait_ge(sem("wT_done"), 7)

            def l0(i, u):
                g = 2 * i + u
                transposed(0, i, u)
                if later(i):
                    pe.wait_ge(sem("asrow_done"), g - 1)
                    pe.wait_ge(sem("adst_done"), g - 1)
                mm(PS[0:1, u, :], watt[:, 0:1], stage2[:, u, 0, :], start=True, stop=True)
                mm(PS[:, 2 + u, :], wdst[:, :], stage2[:, u, 0, :], start=True, stop=True).then_inc(sem("ln0_mm"), 1)
            ahead_loop(pe, lambda i, u: transpose_group(0, i, u), l0)
            pe.wait_ge(sem("aed_loaded"), 16)
            pe.wait_ge(sem("ln_ht"), GROUPS)
            for b in range(RB):
                ins = nc.tensor.transpose(PS[:, 5 + b // 4, (b % 4) * RQ:(b % 4 + 1) * RQ], aed_r[:, b, :], ident[0:RQ, 0:RQ])
            ins.then_inc(sem("aed_tr"), 1)

            pe.wait_ge(sem("logits_split"), 1)
            pe.wait_ge(sem("asrow_done"), GROUPS)
            pe.wait_ge(sem("adst_done"), GROUPS)

            def rows_of_logits(i, s):
                q = 5 * i + s
                pe.wait_ge(sem("hot_made"), q + 1)
                if later(i):
                    pe.wait_ge(sem("picked"), q - 4)
                for j in range(5):
                    for n in range(3):
                        ins = mm(PS[:, s, j * LO:(j + 1) * LO], hot_hi[:, s, j * P:(j + 1) * P], logit_part[:, n, :], start=n == 0, stop=n == 2)
                ins.then_inc(sem("src_mm"), 1)
            for s in range(5):
                rows_of_logits(0, s)
            with pe.Fori(1, 25) as i:
                for s in range(5):
                    rows_of_logits(i, s)

            km = rounds(pe)
            pe.wait_ge(sem("picked"), T // 5)
            with pe.Fori(0, km) as k:
                def turned(g, s):
                    pe.wait_ge(sem("mx_masked"), k * (TP // BATCH) + g + 1)
                    for q in range(4):
                        ins = nc.tensor.transpose(PS[:, s, q * P:(q + 1) * P], pen[:, s, q * P:(q + 1) * P], ident[:, :])
                    ins.then_inc(sem("mx_tr"), 1)

                def spread(g, s):
                    pe.wait_ge(sem("mx_diag"), k * (TP // BATCH) + g + 1)
                    mm(PS[:, 2 + s, :], ones[:, :], diag[:, s, :], start=True, stop=True).then_inc(sem("mx_all"), 1)
                turned(0, 0)
                turned(1, 1)
                spread(0, 0)
                with pe.Fori(1, TP // BATCH // 2) as i:
                    for s in range(2):
                        turned(2 * i + s, s)
                        spread(2 * i + s - 1, (s - 1) % 2)
                spread(TP // BATCH - 1, 1)

            regs = window_regs(pe, "pe")

            def sums(p):
                c = PASS[p]
                C = c["F"] // P
                with pe.Fori(0, km) as k:
                    kk = pe.snap(km * p + k)
                    kr = pe.snap(km * (p - (p > 1)) + k)
                    if c.get("lookup"):
                        pe.wait_ge(sem("round"), (km * 3 + 1) * ROUNDS.index(f"p{p}") + k * 3 + 4)
                        pe.sem_inc(sem("turn"), 1)

                    def types_ready(q):
                        if c.get("lookup"):
                            bases = windows(pe, regs, five(q))
                            pe.wait_ge(sem("toht_made"), k * (T // HALF) + q + 1)
                            pe.sem_inc(sem("turn"), 1)
                            return bases

                    def tile(t, s, slot, use, bases):
                        pe.wait_ge(sem(f"row{slot}"), use * 16)
                        pe.wait_ge(sem("s_ready"), kk * (T + AHEAD) + t + 1)
                        pe.wait_ge(sem("psum_free"), kk * T + t + 1)
                        if c.get("count"):
                            mm(PS[0:RELS, s, 64:64 + WIN], TOH[:, s, :], SEL[:, s, :], start=True, stop=True)
                        if c.get("lookup"):
                            mm(PS[:, s, 64:64 + WIN], TOHT[:, slot // HALF, s * P:(s + 1) * P], cnt8[:, bass.ds(bases[s], WIN)], start=True, stop=True)
                        for ch in range(C):
                            ins = mm(PS[:, s, ch * WIN:(ch + 1) * WIN], ring[:, slot, ch * P:(ch + 1) * P], SEL[:, s, :], start=True, stop=True)
                        if c["ones"]:
                            ins = mm(PS[:, s, WIN:2 * WIN], ones[:, :], SEL[:, s, :], start=True, stop=True)
                        ins.then_inc(sem("mm_done"), 1)
                    with pe.Fori(0, T // 10) as r:
                        for h in range(2):
                            bases = types_ready(2 * r + h)
                            for j in range(HALF):
                                tile(10 * r + h * HALF + j, j, h * HALF + j, kr * (T // 10 + (h == 0)) + r + 1, bases)
                    bases = types_ready(T // HALF - 1)
                    for j in range(HALF):
                        tile(T - HALF + j, j, j, (kr + 1) * (T // 10 + 1), bases)

            def out_x(name, terms_of, bias, bank, ready):
                def body(i, u):
                    g = 2 * i + u
                    pe.wait_ge(sem(name + ready), g + 1)
                    if later(i):
                        pe.wait_ge(sem("x_added"), X_TERMS[name] * GROUPS + g - 1)
                    x_term(name, i, u, terms_of, bias, bank)
                return body

            def x_term(name, i, u, terms_of, bias, bank):
                for q in range(4):
                    dst = PS[:, bank(u), q * P:(q + 1) * P]
                    terms = terms_of(u, q)
                    for n, (lhs, rhs) in enumerate(terms):
                        ins = mm(dst, lhs, rhs, start=n == 0, stop=bias is None and n == len(terms) - 1)
                    if bias is not None:
                        ins = mm(dst, ones[0:1, :], brow[0:1, bias, :], start=False, stop=True)
                ins.then_inc(sem("x_mm"), 1)

            def staged(v, u, ch, q):
                return v[:, u, ch, q * P:(q + 1) * P]

            def degrees(name, i, u):
                g = 2 * i + u
                if later(i) or u:
                    pe.wait_ge(sem("deg_max"), MEANS[name] * GROUPS + g)
                mm(PS[:, 4, :], ones[0:RELS, :], cols(cnt8, g), start=True, stop=True).then_inc(sem("deg"), 1)

            def degrees_after(name, i, u):
                if following(i, u):
                    degrees(name, *following(i, u))

            def root(name, w, i, u, bank_of, src, kc, ready, emptied, lag, before=0, halves=2):
                g = 2 * i + u
                pe.wait_ge(sem(ready), before + g + 1)
                if later(i) or (u and lag == 1):
                    pe.wait_ge(sem(emptied), g + 1 - lag)
                for o in range(halves):
                    for ch in range(kc):
                        lhs = w[:, o * P:(o + 1) * P] if kc == 1 else w[:, ch, o * P:(o + 1) * P]
                        ins = mm(PS[:, bank_of(o), :], lhs, src[:, u, ch, :], start=ch == 0, stop=ch == kc - 1)
                ins.then_inc(sem(name), 1)

            sums(0)
            pe.wait_ge(sem("pass_end"), 1)
            group_loop(pe, out_x("e1", lambda u, q: [(staged(stage, u, 0, q), W0[:, :])], 0, lambda u: 5 + u, "_stage"))
            def l1(i, u):
                g = 2 * i + u
                transposed(1, i, u)
                if later(i):
                    pe.wait_ge(sem("e1_out"), g - 1)
                for q in range(4):
                    ins = mm(PS[:, 2 + u, q * P:(q + 1) * P], staged(stage2, u, 0, q), W1[:, :], start=True, stop=True)
                ins.then_inc(sem("e1_tab"), 1)
            ahead_loop(pe, lambda i, u: transpose_group(1, i, u), l1)
            with pe.Fori(0, km) as k:
                kk = pe.snap(km + k)

                def window_by_source(t, s):
                    pe.wait_ge(sem("s_ready"), kk * (T + AHEAD) + t + 1)
                    mm(PS[0:WIN, s, 0:P], SEL[:, s, :], same[:, s, :], start=True, stop=True).then_inc(sem("b_mm"), 1)

                def tile(t, s, slot, use, last=False):
                    if not last:
                        window_by_source(t + 1, (s + 1) % 5)
                    pe.wait_ge(sem("b_ready"), k * T + t + 1)
                    pe.wait_ge(sem(f"window{slot // 5}"), use * 80)
                    pe.wait_ge(sem("psum_free"), kk * T + t + 1)
                    mm(PS[:, s, P:2 * P], spread_t[:, s, :], ring[0:WIN, slot, D:2 * D], start=True, stop=True).then_inc(sem("mm_done"), 1)
                window_by_source(0, 0)
                with pe.Fori(0, T // 10) as r:
                    for j in range(10):
                        tile(10 * r + j, j % 5, j, k * (T // 10 + (j < 5)) + r + 1)
                for j in range(5):
                    tile(T - 5 + j, j, j, (k + 1) * (T // 10 + 1), j == 4)
            ahead_loop(pe, lambda i, u: transpose_group(2, i, u),
                       lambda i, u: root("ln2_root", Wr1T, i, u, lambda o: 2 * u + o, stage2, 1, "ln_ht", "ln2_rooted", 2, 2 * GROUPS))
            sums(2)
            pe.wait_ge(sem("pass_end"), 3)
            def e3(i, u):
                g = 2 * i + u
                pe.wait_ge(sem("e3_hid"), g + 1)
                for j in range(2):
                    if later(i) or u:
                        pe.wait_ge(sem("e3_out"), 2 * g + j - 1)
                    for q in range(2):
                        for o in range(2):
                            ins = nc.tensor.transpose(PS[:, 5 + j, q * HID + o * P:q * HID + (o + 1) * P],
                                                      staged(stage2, u, o, 2 * j + q), ident[:, :])
                    ins.then_inc(sem("e3_tr"), 1)
                root("e3_hid_mm", Wr2T, i, u, lambda o: 2 * u + o, stage2, 2, "e3_hid", "e3_root", 2)

            def e3_mean(i, u):
                root("e3_mean_mm", Wl1T, i, u, lambda o: 2 * u + o, stage, 1, "e3_stage", "e3_root", 2)
                degrees_after("e3", i, u)
            degrees("e3", 0, 0)
            ahead_loop(pe, e3_mean, e3)
            sums(3)
            pe.wait_ge(sem("pass_end"), 4)
            def e4(i, u):
                g = 2 * i + u
                pe.wait_ge(sem("e4_hid"), g + 1)
                if later(i) or u:
                    pe.wait_ge(sem("e4_out"), g)
                    pe.wait_ge(sem("x_added"), X_TERMS["e4"] * GROUPS + g)
                for q in range(4):
                    for ch in range(2):
                        ins = mm(e4_out[:, q, :], staged(stage2, u, ch, q), W3T[:, ch, :], start=ch == 0, stop=False)
                    ins = mm(e4_out[:, q, D:2 * D], ones[0:1, :], brow[0:1, 1, :], start=False, stop=True)
                ins.then_inc(sem("x_mm"), 1)

            def e4_mean(i, u):
                root("e4_mean_mm", Wl2T, i, u, lambda o: 2 * u + o, stage, 2, "e4_stage", "e4_pre", 2)
                degrees_after("e4", i, u)
            degrees("e4", 0, 0)
            ahead_loop(pe, e4_mean, e4)
            sums(4)
            pe.wait_ge(sem("pass_end"), 5)
            def e5(i, u):
                g = 2 * i + u
                pe.wait_ge(sem("e5_stage"), g + 1)
                if later(i):
                    pe.wait_ge(sem("x_added"), X_TERMS["e5"] * GROUPS + g - 1)
                for q in range(4):
                    ins = nc.tensor.transpose(PS[:, 5 + u, q * P:(q + 1) * P], staged(stage, u, 0, q), ident[:, :])
                ins.then_inc(sem("x_mm"), 1)
            group_loop(pe, e5)

            def units(p, i, u, src):
                kc, halves, width = FIRST_TABLES[p]
                g = 2 * i + u
                per = 4 * halves
                for j in range(per):
                    b, h = j // halves, j % halves
                    if later(i) or u or j >= 2:
                        pe.wait_ge(sem("unit_outa"), UNITS[p] + g * per + j - 1)
                        pe.wait_ge(sem("unit_outd"), UNITS[p] + g * per + j - 1)
                    for n in range(2):
                        at = h * 1024 + n * 512
                        for ch in range(kc):
                            ins = mm(PS[:, 2 * (j % 2) + n, :], staged(src, u, ch, b), relw[:, ch * width + at:ch * width + at + 512],
                                     start=ch == 0, stop=ch == kc - 1)
                    ins.then_inc(sem("unit"), 1)

            pe.wait_ge(sem("relw_loaded"), 16)

            def t5(i, u):
                root("t5_root", root1, i, u, lambda o: 4 + 3 * o, stage2, 1, "ln_ht", "t5_rooted", 1, 3 * GROUPS)
                units(5, i, u, stage2)
            ahead_loop(pe, lambda i, u: transpose_group(3, i, u), t5)
            sums(5)
            pe.wait_ge(sem("relw_loaded"), 48)

            def t6(i, u):
                root("t6_root", root2, i, u, lambda o: 4 + 3 * o, stage2, 2, "t6_hid", "t6_rooted", 1)
                units(6, i, u, stage2)
            group_loop(pe, t6)
            sums(6)
            pe.wait_ge(sem("relw_loaded"), 80)

            def t7(i, u):
                root("t7_root", root3, i, u, lambda o: 4, stage2, 2, "t7_hid", "t7_rooted", 1, halves=1)
                units(7, i, u, stage2)
            group_loop(pe, t7)
            sums(7)
            def e8(i, u):
                g = 2 * i + u
                pe.wait_ge(sem("e8_stage"), g + 1)
                if later(i):
                    pe.wait_ge(sem("x_added"), X_TERMS["e8"] * GROUPS + g - 1)
                for q in range(4):
                    ins = nc.tensor.transpose(PS[:, 5 + u, q * P:(q + 1) * P], staged(stage, u, 0, q), ident[:, :])
                ins.then_inc(sem("x_mm"), 1)
            group_loop(pe, e8)


def kernel(**inputs):
    import numpy as np
    import concourse.bacc as bacc
    from concourse.bass_utils import run_bass_kernel_spmd as run

    nc = bacc.Bacc("TRN2", target_bir_lowering=False, num_devices=1)
    arrays, args = {}, {}
    for name in sorted(inputs):
        v = np.ascontiguousarray(inputs[name])
        arrays["in_" + name] = v
        args[name] = nc.dram_tensor("in_" + name, v.shape, mybir.dt.from_np(v.dtype), kind="ExternalInput").ap()
    out = nc.dram_tensor("out_0", (N, D), F32, kind="ExternalOutput").ap()
    build(nc, args, out)
    return run(nc, [arrays], core_ids=[0]).results[0]["out_0"]
```
